# Optimizing a Trainium2 kernel written in Bass

```python
import numpy as np
import jax
import jax.numpy as jnp

def _softmax(x, axis=-1):
    return jax.nn.softmax(x, axis=axis)

def _gelu(x):
    return jax.nn.gelu(x, approximate=True)

def _silu(x):
    return jax.nn.silu(x)

def _sigmoid(x):
    return jax.nn.sigmoid(x)

def _layernorm(x, axis=-1, eps=1e-05):
    m = jnp.mean(x, axis=axis, keepdims=True)
    v = jnp.var(x, axis=axis, keepdims=True)
    return (x - m) / jnp.sqrt(v + eps)

def _scatter_add(tgt, idx, src, axis=0):
    return tgt.at[idx].add(src)

def _segment_sum(src, seg, n):
    return jax.ops.segment_sum(src, seg, n)
kernel_name = 'mk_gnn_resnorm_d2_gnn_r8_437fa8'

def setup_inputs(seed: int=0):
    np.random.seed(seed)
    _w = jnp.asarray

    def _rec_inputs():
        import jax
        import jax.numpy as jnp
        _gk = jax.random.key(seed)
        x = -0.000202 + 1 * jax.random.normal(jax.random.fold_in(_gk, 1), (12500, 128), jnp.float32)
        src = jax.random.randint(jax.random.fold_in(_gk, 2), (400000,), 0, 12500, jnp.int32)
        dst = jnp.minimum((12500 * jax.random.uniform(jax.random.fold_in(_gk, 3), (400000,)) ** 2.0).astype(jnp.int32), 99999)
        _o = jnp.argsort(dst, stable=True)
        src = src[_o]
        dst = dst[_o]
        edge_attr_64 = 0.000102155 + 1.00015 * jax.random.normal(jax.random.fold_in(_gk, 12), (400000, 64), jnp.float32)
        edge_type_3 = jax.random.randint(jax.random.fold_in(_gk, 14), (400000,), 0, 3, jnp.int32)
        edge_weight = jax.random.uniform(jax.random.fold_in(_gk, 15), (400000,), jnp.float32, 0.0, 0.999998)
        return (x, src, dst, edge_attr_64, edge_type_3, edge_weight)
    x, src, dst, edge_attr_64, edge_type_3, edge_weight = _rec_inputs()

    def _L0_gnn_setup():
        import jax, jax.numpy as jnp
        import numpy as np
        N_NODES = 6250
        N_EDGES = 100000
        IN_FEATS = 128
        OUT_FEATS = 128
        N_REL = 3
        key = jax.random.key(seed)
        k1, k2, k3, k4, k5, k6 = jax.random.split(key, 6)
        feature = jax.random.normal(k1, (N_NODES, IN_FEATS), dtype=jnp.float32)
        bound = float(np.sqrt(6.0 / IN_FEATS))
        weight = jax.random.uniform(k2, (N_REL, IN_FEATS, OUT_FEATS), dtype=jnp.float32, minval=-bound, maxval=bound)
        norm = jax.random.uniform(k3, (N_EDGES,), dtype=jnp.float32)
        src = jax.random.randint(k4, (N_EDGES,), 0, N_NODES)
        dst = jax.random.randint(k5, (N_EDGES,), 0, N_NODES)
        rel_type = jax.random.randint(k6, (N_EDGES,), 0, N_REL)
        return {'feature': feature, 'weight': weight, 'norm': norm, 'src': src, 'dst': dst, 'rel_type': rel_type}
    _L0_gnn_all = _L0_gnn_setup()
    _L0_gnn_in = {k: v for k, v in _L0_gnn_all.items() if k in ('weight',)}
    del _L0_gnn_all

    def _L1_gnn_setup():
        import jax, jax.numpy as jnp
        import numpy as np
        D_NODE = 128
        D_EDGE = 64
        N_NODES = 12500
        N_EDGES = 62500
        key = jax.random.key(seed)
        ks = jax.random.split(key, 12)

        def lin(k, fan_in, fan_out):
            bound = 1.0 / np.sqrt(fan_in)
            kw, kb = jax.random.split(k)
            W = jax.random.uniform(kw, (fan_in, fan_out), jnp.float32, -bound, bound)
            b = jax.random.uniform(kb, (fan_out,), jnp.float32, -bound, bound)
            return (W, b)
        node_features = jax.random.normal(ks[0], (N_NODES, D_NODE), jnp.float32)
        edge_index = jax.random.randint(ks[1], (2, N_EDGES), 0, N_NODES, jnp.int64 if jax.config.jax_enable_x64 else jnp.int32)
        edge_features = jax.random.normal(ks[2], (N_EDGES, D_EDGE), jnp.float32)
        W1, b1 = lin(ks[3], 2 * D_NODE + D_EDGE, D_NODE)
        W2, b2 = lin(ks[4], D_NODE, D_NODE)
        Wg, bg = lin(ks[5], 2 * D_NODE, D_NODE)
        Wt, bt = lin(ks[6], 2 * D_NODE, D_NODE)
        gamma = jnp.ones((D_NODE,), jnp.float32)
        beta = jnp.zeros((D_NODE,), jnp.float32)
        return {'node_features': node_features, 'edge_features': edge_features, 'W1': W1, 'b1': b1, 'W2': W2, 'b2': b2, 'Wg': Wg, 'bg': bg, 'Wt': Wt, 'bt': bt, 'gamma': gamma, 'beta': beta, 'edge_index': edge_index}
    _L1_gnn_all = _L1_gnn_setup()
    _L1_gnn_in = {k: v for k, v in _L1_gnn_all.items() if k in ('W1', 'b1', 'W2', 'b2', 'Wg', 'bg', 'Wt', 'bt', 'gamma', 'beta')}
    del _L1_gnn_all
    return {'x': x, 'src': src, 'dst': dst, 'edge_attr_64': edge_attr_64, 'edge_type_3': edge_type_3, 'edge_weight': edge_weight, 'L0_gnn_weight': _L0_gnn_in['weight'], 'L1_gnn_W1': _L1_gnn_in['W1'], 'L1_gnn_b1': _L1_gnn_in['b1'], 'L1_gnn_W2': _L1_gnn_in['W2'], 'L1_gnn_b2': _L1_gnn_in['b2'], 'L1_gnn_Wg': _L1_gnn_in['Wg'], 'L1_gnn_bg': _L1_gnn_in['bg'], 'L1_gnn_Wt': _L1_gnn_in['Wt'], 'L1_gnn_bt': _L1_gnn_in['bt'], 'L1_gnn_gamma': _L1_gnn_in['gamma'], 'L1_gnn_beta': _L1_gnn_in['beta']}

def reference(x, src, dst, edge_attr_64, edge_type_3, edge_weight, L0_gnn_weight, L1_gnn_W1, L1_gnn_b1, L1_gnn_W2, L1_gnn_b2, L1_gnn_Wg, L1_gnn_bg, L1_gnn_Wt, L1_gnn_bt, L1_gnn_gamma, L1_gnn_beta):
    import jax
    import jax.numpy as jnp

    def _L0_gnn_ref(feature, weight, norm, src, dst, rel_type):
        import jax, jax.numpy as jnp
        import numpy as np
        N_NODES = 6250
        N_EDGES = 100000
        IN_FEATS = 128
        OUT_FEATS = 128
        N_REL = 3
        hr = jnp.einsum('ni,rio->rno', feature, weight)
        msg = hr[rel_type, src] * norm[:, None]
        h = jax.ops.segment_sum(msg, dst, num_segments=feature.shape[0])
        return jax.nn.relu(h)

    def _L1_gnn_ref(node_features, edge_features, W1, b1, W2, b2, Wg, bg, Wt, bt, gamma, beta, edge_index):
        import jax, jax.numpy as jnp
        import numpy as np
        D_NODE = 128
        D_EDGE = 64
        N_NODES = 12500
        N_EDGES = 62500
        num_nodes = node_features.shape[0]
        src, dst = (edge_index[0], edge_index[1])
        h_src = node_features[src]
        h_dst = node_features[dst]
        msg_in = jnp.concatenate([h_src, h_dst, edge_features], axis=-1)
        messages = jax.nn.silu(msg_in @ W1 + b1) @ W2 + b2
        aggregated = jax.ops.segment_sum(messages, dst, num_segments=num_nodes)
        count = jax.ops.segment_sum(jnp.ones((dst.shape[0],), messages.dtype), dst, num_segments=num_nodes)
        aggregated = aggregated / jnp.clip(count, 1.0)[:, None]
        gate_in = jnp.concatenate([node_features, aggregated], axis=-1)
        gate = jax.nn.sigmoid(gate_in @ Wg + bg)
        transform = jnp.tanh(gate_in @ Wt + bt)
        updated = gate * node_features + (1.0 - gate) * transform
        mu = jnp.mean(updated, axis=-1, keepdims=True)
        var = jnp.var(updated, axis=-1, keepdims=True)
        normed = (updated - mu) * jax.lax.rsqrt(var + 1e-05)
        return normed * gamma + beta
    edge_index = jnp.stack([src, dst])
    x = _layernorm(x + _L0_gnn_ref(x, L0_gnn_weight, edge_weight, src, dst, edge_type_3), axis=-1)
    x = _layernorm(x + _L1_gnn_ref(x, edge_attr_64, L1_gnn_W1, L1_gnn_b1, L1_gnn_W2, L1_gnn_b2, L1_gnn_Wg, L1_gnn_bg, L1_gnn_Wt, L1_gnn_bt, L1_gnn_gamma, L1_gnn_beta, edge_index), axis=-1)
    return x

_drawn_inputs = setup_inputs


def setup_inputs(seed=0):
    import zlib

    import numpy as np

    out = dict(_drawn_inputs(seed))
    spreads = {'L1_gnn_gamma': (1.0, 0.2), 'L1_gnn_beta': (0.0, 0.1)}
    factors = {'edge_attr_64': 8.0,
     'L1_gnn_b1': 26.574,
     'L1_gnn_b2': 5.433,
     'L1_gnn_bg': 6.386,
     'L1_gnn_bt': 3.889}
    for name, (base, spread) in spreads.items():
        noise = np.random.default_rng([zlib.crc32(name.encode()), seed]).standard_normal(out[name].shape)
        drawn = base * np.exp(spread * noise) if base else spread * noise
        out[name] = jnp.asarray(drawn.astype(out[name].dtype))
    for name, factor in factors.items():
        out[name] = (out[name] * factor).astype(out[name].dtype)
    return out
```

```python
from contextlib import ExitStack

import concourse.bass as bass
from concourse import mybir

ALU = mybir.AluOpType
ACT = mybir.ActivationFunctionType
AX = mybir.AxisListType
F32 = mybir.dt.float32
I32 = mybir.dt.int32
BF16 = mybir.dt.bfloat16
RMAX = bass.bass_isa.ReduceOp.max

P = 128
NODES = 12500
EDGES = 400000
D = 128
DE = 64
NREL = 3
EPS = 1e-5
BLOCKS = -(-NODES // P)
NPAD = BLOCKS * P
GROUP = 8
GE = GROUP * P
STEPS = 8
HALF = 4
HC = HALF * GROUP
GROUPS = -(-EDGES // (GE * STEPS)) * STEPS
BODIES = GROUPS // STEPS
HALVES = GROUPS // HALF
EPAD = GROUPS * GE
TILES = EPAD // P
RING = 4
CH = 7
CHUNKS = BLOCKS // CH
UW = D + 1
BANK = 512
CREDIT = P


def ds(i, n=1):
    return bass.ds(i, n)


def wait_apart(eng, sem, value, passed):
    eng.wait_ge(sem, value)
    eng.sem_inc(passed, 1)


class Build:

    def __init__(self, nc, stack):
        self.nc, self.stack = nc, stack

    def sb(self, name, shape, dt=F32):
        return self.stack.enter_context(self.nc.sbuf_tensor(name, shape, dt))

    def sem(self, name):
        return self.stack.enter_context(self.nc.semaphore(name))


def block_range(nc, eng, rng, g):
    word = eng.value_load(rng[0:1, ds(g + 1)], min_val=0, max_val=2 ** 31 - 1)
    why = "phase_tables clamps blocks to those there are, and their number bounds the count"
    return tuple(nc.s_assert_within(eng.snap(v), 0, most, skip_runtime_bounds_check_because=why)
                 for v, most in ((word % P, BLOCKS - 1), (word // P % P, BLOCKS - 1),
                                 (word // (P * P), GROUPS * BLOCKS + CREDIT)))


def phase_tables(nc, keep, xT, w0, dst_tiles, dst_rows, hr, ab):
    rng, HU = keep["rng"], keep["HU"]
    iota_row, neg_kb, node_id, ones2 = keep["iota_row"], keep["neg_kb"], keep["node_id"], keep["ones2"]
    ps = keep["ps"]
    with ExitStack() as stack:
        b = Build(nc, stack)
        w0_sb = b.sb("w0_sb", [P, NREL * D])
        xT_sb = [b.sb(f"xT_sb{i}", [P, CH * P]) for i in range(2)]
        stage = [b.sb(f"hr_stage{i}", [P, CH, NREL * D]) for i in range(2)]
        dst_i = b.sb("dst_i", [P, TILES], I32)
        dst_r = b.sb("dst_r", [P, TILES], I32)
        low_i = b.sb("low_i", [P, TILES], I32)
        ab_sb = b.sb("ab_sb", [P, 2, TILES], BF16)
        ext = b.sb("ext", [P, 2, GROUPS])
        ext_all = b.sb("ext_all", [P, 2, GROUPS])
        lohi_i = b.sb("lohi_i", [1, 2, GROUPS], I32)
        lohi = b.sb("lohi", [1, 2, GROUPS])
        one_row = b.sb("one_row", [1, GROUPS])
        extras = b.sb("extras", [1, GROUPS])
        low_bits, high_bits = b.sb("low_bits", [1, GROUPS], I32), b.sb("high_bits", [1, GROUPS], I32)
        upto = b.sb("upto", [1, GROUPS])
        kb_i = b.sb("kb_i", [P, BLOCKS + 1], I32)
        io_i = b.sb("io_i", [P, P], I32)

        w0_loaded = b.sem("w0_loaded")
        dst_loaded, rows_loaded = b.sem("dst_loaded"), b.sem("rows_loaded")
        xT_loaded = [b.sem(f"xT_loaded{i}") for i in range(2)]
        hr_stored = [b.sem(f"hr_stored{i}") for i in range(2)]
        ab_stored = b.sem("ab_stored")
        mm_done = b.sem("mm_done")
        act_out = b.sem("act_out")
        dve_out = b.sem("dve_out")
        v_chain = b.sem("v_chain")
        ab_ready = b.sem("ab_ready")
        ext_ready, ext_reduced = b.sem("ext_ready"), b.sem("ext_reduced")
        iotas, const_done = b.sem("iotas"), b.sem("const_done")
        EV, OD = (CH + 1) // 2, CH // 2
        passed = keep["passed"]
        block = stack.enter_context(nc.Block())

        @block.sync
        def _(sp):
            sp.dma_start(w0_sb[:, :], w0).then_inc(w0_loaded, 16)
            sp.dma_start(dst_i[:, :], dst_tiles).then_inc(dst_loaded, 16)
            sp.dma_start(dst_r[:, :], dst_rows).then_inc(rows_loaded, 16)
            with sp.Fori(0, CHUNKS // 2) as i:
                for s in range(2):
                    sp.wait_ge(mm_done, CH * (2 * i + s + 1))
                    sp.dma_start(xT_sb[s][:, :], xT[:, ds((2 * i + s) * CH * P, CH * P)]).then_inc(xT_loaded[s], 16)
            sp.wait_ge(ab_ready, 1)
            sp.dma_start(ab.rearrange("a (p n) -> p a n", p=P), ab_sb[:, :, :]).then_inc(ab_stored, 16)
            sp.wait_ge(ab_stored, 16)

        @block.gpsimd
        def _(pool):
            nc.gpsimd.iota(kb_i[:, :], pattern=[[-P, BLOCKS + 1]], base=0, channel_multiplier=0).then_inc(iotas, 1)
            nc.gpsimd.iota(io_i[:, :], pattern=[[1, P]], base=0, channel_multiplier=0).then_inc(iotas, 1)
            nc.gpsimd.memset(HU[:, :], 0.0)
            nc.gpsimd.memset(ones2[:, :], 1.0)
            nc.gpsimd.memset(keep["ident"][:, :], 0.0).then_inc(iotas, 1)
            pool.wait_ge(iotas, 3)
            nc.gpsimd.affine_select(out=keep["ident"][:, :], in_=keep["ident"][:, :], compare_op=ALU.not_equal,
                                    fill=1.0, base=0, pattern=[[-1, P]], channel_multiplier=1).then_inc(iotas, 1)
            nc.gpsimd.iota(keep["pid_i"][:, :], pattern=[[P, BLOCKS]], base=0, channel_multiplier=1).then_inc(iotas, 1)
            pool.wait_ge(ext_ready, 1)
            nc.gpsimd.partition_all_reduce(ext_all[:, :, :].rearrange("p a g -> p (a g)"),
                                           ext[:, :, :].rearrange("p a g -> p (a g)"), P, RMAX).then_inc(ext_reduced, 1)

        @block.tensor
        def _(pe):
            pe.sem_inc(mm_done, 2 * CH)
            pe.wait_ge(w0_loaded, 16)
            with pe.Fori(0, CHUNKS // 2) as i:
                for s in range(2):
                    c = 2 * i + s
                    pe.wait_ge(xT_loaded[s], 16 * (i + 1))
                    for j in range(CH):
                        if j % 2 == 0:
                            pe.wait_ge(act_out, EV * c + j // 2 + 1)
                        else:
                            pe.wait_ge(dve_out, OD * c + j // 2 + 1)
                        nc.tensor.matmul(ps[:, 512 * j:512 * j + NREL * D], xT_sb[s][:, j * P:(j + 1) * P],
                                         w0_sb[:, :], start=True, stop=True).then_inc(mm_done, 1)

        @block.scalar
        def _(act):
            act.sem_inc(act_out, EV)
            with act.Fori(0, CHUNKS // 2) as i:
                for s in range(2):
                    c = 2 * i + s
                    act.wait_ge(hr_stored[s], 16 * (i + 1))
                    for j in range(0, CH, 2):
                        act.wait_ge(mm_done, 2 * CH + CH * c + j + 1)
                        nc.scalar.activation(stage[s][:, j, :], ps[:, 512 * j:512 * j + NREL * D],
                                             ACT.Copy).then_inc(act_out, 1)
                    act.wait_ge(act_out, EV * (c + 2))
                    act.wait_ge(dve_out, OD * (c + 2))
                    act.dma_start(hr[ds(c * CH * P * NREL, CH * P * NREL), :].rearrange("(j p r) f -> p j (r f)", p=P, r=NREL),
                                  stage[s][:, :, :]).then_inc(hr_stored[s], 16)
            for s in range(2):
                act.wait_ge(hr_stored[s], 16 * (CHUNKS // 2 + 1))

        @block.vector
        def _(dve):
            dve.sem_inc(dve_out, OD)
            for s in range(2):
                dve.sem_inc(hr_stored[s], 16)
            dve.wait_ge(dst_loaded, 16)
            groups = dst_i[:, :].rearrange("p (g u) -> p g u", u=GROUP)
            nc.vector.tensor_reduce(ext[:, 0, :], groups, axis=AX.X, op=ALU.max).then_inc(v_chain, 1)
            nc.vector.tensor_reduce(ext[:, 1, :], groups, axis=AX.X, op=ALU.min).then_inc(v_chain, 1)
            dve.wait_ge(v_chain, 2)
            nc.vector.tensor_scalar(ext[:, 1, :], ext[:, 1, :], -1.0, None, ALU.mult).then_inc(ext_ready, 1)
            dve.wait_ge(rows_loaded, 16)
            nc.vector.tensor_scalar(low_i[:, :], dst_r[:, :], P - 1, None, ALU.bitwise_and).then_inc(v_chain, 1)
            dve.wait_ge(v_chain, 3)
            nc.vector.tensor_tensor(ab_sb[:, 0, :], dst_r[:, :], low_i[:, :], ALU.subtract)
            nc.vector.tensor_copy(ab_sb[:, 1, :], low_i[:, :]).then_inc(ab_ready, 1)
            dve.wait_ge(iotas, 5)
            nc.vector.tensor_copy(neg_kb[:, :], kb_i[:, :])
            nc.vector.tensor_copy(iota_row[:, :], io_i[:, :])
            nc.vector.tensor_copy(node_id[:, :], keep["pid_i"][:, :])
            nc.vector.memset(keep["eps"][:, :], EPS)
            dve.wait_ge(ext_reduced, 1)
            nc.vector.tensor_copy(lohi_i[0:1, 0, :], ext_all[0:1, 0, :])
            nc.vector.tensor_scalar(lohi_i[0:1, 1, :], ext_all[0:1, 1, :], -1.0, None, ALU.mult).then_inc(v_chain, 1)
            nc.vector.memset(one_row[:, :], 1.0).then_inc(v_chain, 1)
            dve.wait_ge(v_chain, 5)
            nc.vector.tensor_scalar(lohi_i[:, :, :], lohi_i[:, :, :], 7, None, ALU.arith_shift_right).then_inc(v_chain, 1)
            dve.wait_ge(v_chain, 6)
            nc.vector.tensor_scalar(lohi[:, :, :], lohi_i[:, :, :], 0.0, float(BLOCKS - 1), ALU.max, ALU.min).then_inc(v_chain, 1)
            dve.wait_ge(v_chain, 7)
            nc.vector.scalar_tensor_tensor(out=low_bits[:, :], in0=lohi[:, 0, :], scalar=float(P), in1=lohi[:, 1, :],
                                           op0=ALU.mult, op1=ALU.add)
            nc.vector.tensor_tensor(extras[:, :], lohi[:, 0, :], lohi[:, 1, :], ALU.subtract).then_inc(v_chain, 1)
            dve.wait_ge(v_chain, 8)
            nc.vector.tensor_tensor_scan(upto[:, :], one_row[:, :], extras[:, :], 0.0, ALU.mult, ALU.add).then_inc(v_chain, 1)
            dve.wait_ge(v_chain, 9)
            nc.vector.scalar_tensor_tensor(out=high_bits[:, :], in0=upto[:, :], scalar=float(CREDIT), in1=lohi[:, 0, :],
                                           op0=ALU.add, op1=ALU.subtract).then_inc(v_chain, 1)
            dve.wait_ge(v_chain, 10)
            nc.vector.tensor_scalar(high_bits[:, :], high_bits[:, :], 14, None, ALU.arith_shift_left).then_inc(v_chain, 1)
            dve.wait_ge(v_chain, 11)
            nc.vector.tensor_tensor(rng[0:1, 1:], high_bits[:, :], low_bits[:, :], ALU.bitwise_or)
            with dve.Fori(0, CHUNKS // 2) as i:
                for s in range(2):
                    c = 2 * i + s
                    dve.wait_ge(hr_stored[s], 16 * (i + 1))
                    for j in range(1, CH, 2):
                        dve.wait_ge(mm_done, 2 * CH + CH * c + j + 1)
                        nc.vector.tensor_copy(stage[s][:, j, :], ps[:, 512 * j:512 * j + NREL * D]).then_inc(dve_out, 1)


def phase_relational(nc, keep, meta, wts, hr):
    rng, HU, iota_row, neg_kb, ps = keep["rng"], keep["HU"], keep["iota_row"], keep["neg_kb"], keep["ps"]
    with ExitStack() as stack:
        b = Build(nc, stack)
        meta_sb = [b.sb(f"meta_sb{i}", [P, 3, HC], I32) for i in range(2)]
        w_sb = [b.sb(f"w_sb{i}", [P, HC]) for i in range(2)]
        idx = [b.sb(f"idx{i}", [P, HC], I32) for i in range(2)]
        dstf = [b.sb(f"dstf{i}", [P, HC]) for i in range(2)]
        rel = [b.sb(f"rel{i}", [P, GROUP]) for i in range(2)]
        rel_x = b.sb("rel_x", [P, GROUP])
        S = [b.sb(f"S{i}", [P, GE]) for i in range(2)]
        S_x = b.sb("S_x", [P, GE])
        G = [b.sb(f"G{i}", [P, GE]) for i in range(RING)]
        acc, acc_x = ps[:, 0:D], ps[:, 512:512 + D]

        meta_loaded = [b.sem(f"meta_loaded{i}") for i in range(2)]
        w_loaded = [b.sem(f"w_loaded{i}") for i in range(2)]
        idx_ready = b.sem("idx_ready")
        gathered = [b.sem(f"gathered{i}") for i in range(RING)]
        s_ready, agg_done = b.sem("s_ready"), b.sem("agg_done")
        acc_free = b.sem("acc_free")
        sx_ready, aggx_done = b.sem("sx_ready"), b.sem("aggx_done")
        rel_ready, relx_ready = b.sem("rel_ready"), b.sem("relx_ready")
        addx_done = b.sem("addx_done")
        step_done = b.sem("step_done")
        passed = keep["passed"]
        block = stack.enter_context(nc.Block())

        @block.gpsimd
        def _(pool):
            with pool.Fori(0, BODIES) as i:
                for s in range(STEPS):
                    g = STEPS * i + s
                    if s % HALF == 0:
                        pool.wait_ge(idx_ready, 2 * i + s // HALF + 1)
                    wait_apart(pool, step_done, g + 3, passed)
                    for u in range(GROUP):
                        col = (s % HALF) * GROUP + u
                        nc.gpsimd.indirect_dma_start(
                            out=G[s % RING][:, u * P:(u + 1) * P], out_offset=None, in_=hr,
                            in_offset=bass.IndirectOffsetOnAxis(ap=idx[s // HALF][:, col:col + 1], axis=0),
                        ).then_inc(gathered[s % RING], 16)

        @block.scalar
        def _(act):
            def load(h, m):
                act.dma_start(meta_sb[m][:, :, :], meta[ds(h), :, :, :].rearrange("o p a c -> (o p) a c")).then_inc(meta_loaded[m], 16)
                act.dma_start(w_sb[m][:, :], wts[ds(h), :, :].rearrange("o p c -> (o p) c")).then_inc(w_loaded[m], 16)

            load(0, 0)
            with act.Fori(0, BODIES) as i:
                for m in range(2):
                    act.wait_ge(step_done, RING + 1 + STEPS * i + HALF * m + 1)
                    load(2 * i + m + 1, 1 - m)

        @block.vector
        def _(dve):
            def prepare(h, m, times):
                dve.wait_ge(meta_loaded[m], 16 * times)
                dve.wait_ge(w_loaded[m], 16 * times)
                nc.vector.scalar_tensor_tensor(out=idx[m][:, :], in0=meta_sb[m][:, 0, :], scalar=float(NREL),
                                               in1=meta_sb[m][:, 1, :], op0=ALU.mult, op1=ALU.add).then_inc(idx_ready, 1)
                nc.vector.tensor_copy(dstf[m][:, :], meta_sb[m][:, 2, :]).then_inc(dst_ready, 1)

            def one_hot(out, rel_t, ready, count, k, s):
                m, c0 = s // HALF, (s % HALF) * GROUP
                nc.vector.tensor_scalar(rel_t[:, :], dstf[m][:, c0:c0 + GROUP], neg_kb[:, ds(k)], None,
                                        ALU.add).then_inc(ready, 1)
                dve.wait_ge(ready, count)
                for u in range(GROUP):
                    last = nc.vector.tensor_scalar(out[:, u * P:(u + 1) * P], iota_row[:, :], rel_t[:, u:u + 1],
                                                   w_sb[m][:, c0 + u:c0 + u + 1], ALU.is_equal, ALU.mult)
                return last

            def back(g, s):
                lo, hi, base = block_range(nc, dve, rng, g)
                dve.wait_ge(agg_done, g + 1)
                nc.vector.tensor_tensor(HU[:, ds(lo * UW, D)], HU[:, ds(lo * UW, D)], acc, ALU.add).then_inc(acc_free, 1)
                with dve.If(lo < hi):
                    with dve.Fori(lo + 1, hi + 1) as k:
                        one_hot(S_x, rel_x, relx_ready, base + k, k, s).then_inc(sx_ready, 1)
                        dve.wait_ge(aggx_done, base + k)
                        nc.vector.tensor_tensor(HU[:, ds(k * UW, D)], HU[:, ds(k * UW, D)], acc_x, ALU.add).then_inc(addx_done, 1)
                        wait_apart(dve, addx_done, base + k, passed)

            dst_ready = keep["dst_ready0"]
            dve.sem_inc(acc_free, 1)
            dve.sem_inc(relx_ready, CREDIT)
            dve.sem_inc(sx_ready, CREDIT)
            dve.sem_inc(addx_done, CREDIT)
            dve.sem_inc(step_done, RING + 1)
            prepare(0, 0, 1)
            with dve.Fori(0, BODIES) as i:
                for s in range(STEPS):
                    g = STEPS * i + s
                    if s % HALF == 0:
                        dve.wait_ge(dst_ready, 2 * i + s // HALF + 1)
                    lo, hi, base = block_range(nc, dve, rng, g)
                    one_hot(S[s % 2], rel[s % 2], rel_ready, g + 1, lo, s).then_inc(s_ready, 1)
                    if s == 0:
                        with dve.If(i > 0):
                            back(g - 1, STEPS - 1)
                    else:
                        back(g - 1, s - 1)
                    if s % HALF == 2:
                        m = s // HALF
                        prepare(None, 1 - m, i + 1 + m)
                    dve.drain().then_inc(step_done, 1)
            back(GROUPS - 1, STEPS - 1)

        @block.tensor
        def _(pe):
            pe.sem_inc(aggx_done, CREDIT)

            def aggregate(out, onehot, s):
                for u in range(GROUP):
                    last = nc.tensor.matmul(out, onehot[:, u * P:(u + 1) * P], G[s % RING][:, u * P:(u + 1) * P],
                                            start=(u == 0), stop=(u == GROUP - 1))
                return last

            with pe.Fori(0, BODIES) as i:
                for s in range(STEPS):
                    g = STEPS * i + s
                    lo, hi, base = block_range(nc, pe, rng, g)
                    pe.wait_ge(s_ready, g + 1)
                    pe.wait_ge(gathered[s % RING], 16 * GROUP * (STEPS // RING * i + s // RING + 1))
                    pe.wait_ge(acc_free, g + 1)
                    aggregate(acc, S[s % 2], s).then_inc(agg_done, 1)
                    with pe.If(lo < hi):
                        with pe.Fori(lo + 1, hi + 1) as k:
                            pe.wait_ge(sx_ready, base + k)
                            aggregate(acc_x, S_x, s).then_inc(aggx_done, 1)


def layer_norm_stats(nc, eng, src, stats, mv, chain, n0, passed):
    for j in range(CH):
        last = nc.vector.bn_stats(stats[:, j, :], src[:, j, :])
    last.then_inc(chain, 1)
    wait_apart(eng, chain, n0 + 1, passed)
    for j in range(CH):
        last = nc.vector.bn_aggr(mv[:, j, :], stats[:, j, :])
    last.then_inc(chain, 1)


def phase_nodes(nc, keep, x, w1sd, b1, x1, x1T, hs):
    HU, Hd, ps, ident, eps = keep["HU"], keep["Hd"], keep["ps"], keep["ident"], keep["eps"]
    with ExitStack() as stack:
        b = Build(nc, stack)
        w_sb = b.sb("w1sd_sb", [P, 2 * D])
        b1_sb = b.sb("b1_sb", [P, D])
        xc = [b.sb(f"xc{i}", [P, CH, D]) for i in range(2)]
        x1T_sb = [b.sb(f"x1T_sb{i}", [P, CH * P]) for i in range(2)]
        hs_sb = [b.sb(f"hs_sb{i}", [P, CH, D]) for i in range(2)]
        stats = b.sb("stats", [P, CH, 6])
        mv = b.sb("mv", [P, CH, 2])
        sd = b.sb("sd", [P, CH])
        zeros = b.sb("zeros", [P, CH * UW])
        tps = ps[:, 0:CH * P]
        hs_ps = ps[:, 1024:1024 + CH * D].rearrange("p (j n) -> p j n", j=CH)
        hd_ps = ps[:, 2048:2048 + CH * D].rearrange("p (j n) -> p j n", j=CH)

        w_loaded = b.sem("w1_loaded")
        x_loaded = [b.sem(f"x_loaded{i}") for i in range(2)]
        x1_stored = [b.sem(f"x1_stored{i}") for i in range(2)]
        x1T_stored = [b.sem(f"x1T_stored{i}") for i in range(2)]
        hs_stored = [b.sem(f"hs_stored{i}") for i in range(2)]
        chain = b.sem("chain")
        sd_done = b.sem("sd_done")
        x1_ready = b.sem("x1_ready")
        t_done, xT_ready = b.sem("t_done"), b.sem("xT_ready")
        h_done = b.sem("h_done")
        hs_ready, hd_done = b.sem("hs_ready"), b.sem("hd_done")
        zeroed = b.sem("zeroed")
        CHAIN = 4
        passed = keep["passed"]
        block = stack.enter_context(nc.Block())

        def rows(dram, c):
            return dram[ds(c * CH * P, CH * P), :].rearrange("(j p) f -> p j f", p=P)

        @block.sync
        def _(sp):
            sp.dma_start(w_sb[:, :], w1sd).then_inc(w_loaded, 16)
            sp.dma_start(b1_sb[:, :], b1.to_broadcast([P, D])).then_inc(w_loaded, 16)
            for s in range(2):
                sp.sem_inc(x1_stored[s], 16)
                sp.sem_inc(x1T_stored[s], 16)
                sp.sem_inc(hs_stored[s], 16)
            with sp.Fori(0, CHUNKS // 2) as i:
                for s in range(2):
                    wait_apart(sp, x1_stored[s], 16 * (i + 1), passed)
                    wait_apart(sp, t_done, 2 * i + s + 1, passed)
                    sp.dma_start(xc[s][:, :, :], rows(x, 2 * i + s)).then_inc(x_loaded[s], 16)

        @block.gpsimd
        def _(pool):
            nc.gpsimd.memset(zeros[:, :], 0.0).then_inc(zeroed, 1)
            pool.wait_ge(zeroed, 1)
            with pool.Fori(0, CHUNKS) as c:
                pool.wait_ge(chain, CHAIN * c + 1)
                nc.gpsimd.tensor_copy(HU[:, ds(c * CH * UW, CH * UW)], zeros[:, :]).then_inc(zeroed, 1)

        @block.vector
        def _(dve):
            with dve.Fori(0, CHUNKS // 2) as i:
                for s in range(2):
                    c = 2 * i + s
                    dve.wait_ge(x_loaded[s], 16 * (i + 1))
                    hu = HU[:, ds(c * CH * UW, CH * UW)].rearrange("p (j n) -> p j n", j=CH)[:, :, 0:D]
                    nc.vector.scalar_tensor_tensor(out=xc[s][:, :, :], in0=hu, scalar=0.0, in1=xc[s][:, :, :],
                                                   op0=ALU.max, op1=ALU.add).then_inc(chain, 1)
                    dve.wait_ge(chain, CHAIN * c + 1)
                    layer_norm_stats(nc, dve, xc[s], stats, mv, chain, CHAIN * c + 1, passed)
                    dve.wait_ge(sd_done, c + 1)
                    nc.vector.reciprocal(sd[:, :], sd[:, :]).then_inc(chain, 1)
                    dve.wait_ge(chain, CHAIN * c + 4)
                    for j in range(CH):
                        last = nc.vector.tensor_scalar(xc[s][:, j, :], xc[s][:, j, :], mv[:, j, 0:1], sd[:, j:j + 1],
                                                       ALU.subtract, ALU.mult)
                    last.then_inc(x1_ready, 1)
                    dve.wait_ge(w_loaded, 32)
                    dve.wait_ge(h_done, c + 1)
                    hd = Hd[:, ds(c * CH * D, CH * D)].rearrange("p (j n) -> p j n", j=CH)
                    bias = b1_sb[:, :].rearrange("p (o f) -> p o f", o=1).to_broadcast([P, CH, D])
                    nc.vector.tensor_tensor(hd, hd_ps, bias, ALU.add).then_inc(hd_done, 1)

        @block.scalar
        def _(act):
            with act.Fori(0, CHUNKS // 2) as i:
                for s in range(2):
                    c = 2 * i + s
                    act.wait_ge(chain, CHAIN * c + 3)
                    nc.scalar.activation(sd[:, :], mv[:, :, 1], ACT.Sqrt, bias=eps[:, :]).then_inc(sd_done, 1)
                    act.wait_ge(x1_ready, c + 1)
                    act.dma_start(rows(x1, c), xc[s][:, :, :]).then_inc(x1_stored[s], 16)
                    act.wait_ge(t_done, 2 + c + 1)
                    act.wait_ge(x1T_stored[s], 16 * (i + 1))
                    nc.scalar.activation(x1T_sb[s][:, :], tps, ACT.Copy).then_inc(xT_ready, 1)
                    act.wait_ge(xT_ready, c + 1)
                    act.dma_start(x1T[:, ds(c * CH * P, CH * P)], x1T_sb[s][:, :]).then_inc(x1T_stored[s], 16)
                    act.wait_ge(h_done, c + 1)
                    act.wait_ge(hs_stored[s], 16 * (i + 1))
                    nc.scalar.activation(hs_sb[s][:, :, :], hs_ps, ACT.Copy).then_inc(hs_ready, 1)
                    act.wait_ge(hs_ready, c + 1)
                    act.dma_start(rows(hs, c), hs_sb[s][:, :, :]).then_inc(hs_stored[s], 16)
            for s in range(2):
                act.wait_ge(x1_stored[s], 16 * (CHUNKS // 2 + 1))
                act.wait_ge(x1T_stored[s], 16 * (CHUNKS // 2 + 1))
                act.wait_ge(hs_stored[s], 16 * (CHUNKS // 2 + 1))

        @block.tensor
        def _(pe):
            pe.sem_inc(t_done, 2)
            pe.wait_ge(w_loaded, 32)
            with pe.Fori(0, CHUNKS // 2) as i:
                for s in range(2):
                    c = 2 * i + s
                    pe.wait_ge(x1_ready, c + 1)
                    for j in range(CH):
                        last = nc.tensor.transpose(tps[:, j * P:(j + 1) * P], xc[s][:, j, :], ident[:, :])
                    last.then_inc(t_done, 1)
                    pe.wait_ge(xT_ready, c + 1)
                    for j in range(CH):
                        xT = x1T_sb[s][:, j * P:(j + 1) * P]
                        nc.tensor.matmul(hs_ps[:, j, :], xT, w_sb[:, 0:D], start=True, stop=True)
                        last = nc.tensor.matmul(hd_ps[:, j, :], xT, w_sb[:, D:2 * D], start=True, stop=True)
                    last.then_inc(h_done, 1)


def phase_messages(nc, keep, meta, edges, ab, w1e, hs):
    rng, HU, Hd, iota_row = keep["rng"], keep["HU"], keep["Hd"], keep["iota_row"]
    neg_kb, node_id, ones2, ps = keep["neg_kb"], keep["node_id"], keep["ones2"], keep["ps"]
    with ExitStack() as stack:
        b = Build(nc, stack)
        w1e_sb = b.sb("w1e_sb", [P, 2 * D])
        meta_sb = [b.sb(f"mmeta_sb{i}", [P, 3, HC], I32) for i in range(2)]
        dstf = [b.sb(f"mdstf{i}", [P, HC]) for i in range(2)]
        ea = [b.sb(f"ea{i}", [P, GE // 2]) for i in range(RING)]
        ab_sb = [b.sb(f"mab{i}", [P, GE], BF16) for i in range(RING)]
        S = [b.sb(f"mS{i}", [P, GE]) for i in range(2)]
        S_x = b.sb("mS_x", [P, GE])
        rel = [b.sb(f"mrel{i}", [P, GROUP]) for i in range(2)]
        rel_x = b.sb("mrel_x", [P, GROUP])
        ST = b.sb("ST", [P, GE])
        ST_x = b.sb("ST_x", [P, GE])
        G = [b.sb(f"mG{i}", [P, GE]) for i in range(RING)]
        pre = [b.sb(f"pre{i}", [P, GE]) for i in range(2)]
        A = [b.sb(f"A{i}", [P, GROUP, UW]) for i in range(2)]
        h_ps = [ps[:, 0:GE], ps[:, GE:2 * GE]]
        bc = ps[:, 2 * GE:3 * GE]
        acc, acc_x = ps[:, 3 * GE:3 * GE + UW], ps[:, 3 * GE + 512:3 * GE + 512 + UW]

        w_loaded = b.sem("w1e_loaded")
        meta_loaded = [b.sem(f"mmeta_loaded{i}") for i in range(2)]
        dst_ready = b.sem("mdst_ready")
        ea_loaded = [b.sem(f"ea_loaded{i}") for i in range(RING)]
        ab_loaded = [b.sem(f"ab_loaded{i}") for i in range(RING)]
        ea_used = b.sem("ea_used")
        gathered = [b.sem(f"mgathered{i}") for i in range(RING)]
        bc_ready = b.sem("bc_ready")
        st_ready, h_ready = b.sem("st_ready"), b.sem("h_ready")
        s_ready = b.sem("ms_ready")
        h_added = b.sem("h_added")
        silu_done = b.sem("silu_done")
        agg_done = b.sem("magg_done")
        acc_free = b.sem("macc_free")
        stx_ready, hx_done = b.sem("stx_ready"), b.sem("hx_done")
        sx_ready, aggx_done = b.sem("msx_ready"), b.sem("maggx_done")
        rel_ready, relx_ready = b.sem("mrel_ready"), b.sem("mrelx_ready")
        addx_done = b.sem("maddx_done")
        a_ones, ab_zeroed, w_zeroed = b.sem("a_ones"), b.sem("ab_zeroed"), b.sem("w_zeroed")
        passed = keep["passed"]
        block = stack.enter_context(nc.Block())

        @block.gpsimd
        def _(pool):
            with pool.Fori(0, BODIES) as i:
                for s in range(STEPS):
                    g = STEPS * i + s
                    if s % HALF == 0:
                        m = s // HALF
                        pool.wait_ge(meta_loaded[m], 16 * (i + 1))
                    wait_apart(pool, h_added, g + 1, passed)
                    for u in range(GROUP):
                        col = (s % HALF) * GROUP + u
                        nc.gpsimd.indirect_dma_start(
                            out=G[s % RING][:, u * P:(u + 1) * P], out_offset=None, in_=hs,
                            in_offset=bass.IndirectOffsetOnAxis(ap=meta_sb[s // HALF][:, 0, col:col + 1], axis=0),
                        ).then_inc(gathered[s % RING], 16)

        @block.sync
        def _(sp):
            sp.wait_ge(w_zeroed, 1)
            for half in range(2):
                sp.dma_start(w1e_sb[half * DE:(half + 1) * DE, half * D:(half + 1) * D], w1e).then_inc(w_loaded, 16)
            sp.wait_ge(ab_zeroed, RING)
            with sp.Fori(0, BODIES) as i:
                for s in range(STEPS):
                    g = STEPS * i + s
                    sp.wait_ge(ea_used, g + 1)
                    sp.dma_start(ea[s % RING][:, :], edges[ds(g), :, :].rearrange("o p e -> (o p) e")).then_inc(ea_loaded[s % RING], 16)
                    sp.dma_start(ab_sb[s % RING][0:2, :], ab[:, ds(g * GE, GE)]).then_inc(ab_loaded[s % RING], 16)

        @block.scalar
        def _(act):
            def load(h, m):
                act.dma_start(meta_sb[m][:, :, :], meta[ds(h), :, :, :].rearrange("o p a c -> (o p) a c")).then_inc(meta_loaded[m], 16)

            load(0, 0)
            act.sem_inc(silu_done, 2)
            act.wait_ge(a_ones, 2)
            with act.Fori(0, BODIES) as i:
                for s in range(STEPS):
                    g = STEPS * i + s
                    act.wait_ge(h_added, RING + g + 1)
                    nc.scalar.activation(A[s % 2][:, :, 0:D], pre[s % 2][:, :].rearrange("p (u f) -> p u f", u=GROUP),
                                         ACT.Silu).then_inc(silu_done, 1)
                    if s % HALF == 1:
                        m = s // HALF
                        load(2 * i + m + 1, 1 - m)

        @block.vector
        def _(dve):
            def prepare(m, times):
                dve.wait_ge(meta_loaded[m], 16 * times)
                nc.vector.tensor_copy(dstf[m][:, :], meta_sb[m][:, 2, :]).then_inc(dst_ready, 1)

            def one_hot(out, rel_t, ready, count, k, s):
                m, c0 = s // HALF, (s % HALF) * GROUP
                nc.vector.tensor_scalar(rel_t[:, :], dstf[m][:, c0:c0 + GROUP], neg_kb[:, ds(k)], None,
                                        ALU.add).then_inc(ready, 1)
                dve.wait_ge(ready, count)
                nodes = iota_row[:, :].rearrange("p (o n) -> p o n", o=1).to_broadcast([P, GROUP, P])
                dsts = rel_t[:, :].rearrange("p (u o) -> p u o", o=1).to_broadcast([P, GROUP, P])
                return nc.vector.tensor_tensor(out[:, :].rearrange("p (u n) -> p u n", u=GROUP), nodes, dsts, ALU.is_equal)

            def one_hot_T(out, k):
                return nc.vector.tensor_scalar(out[:, :], bc, node_id[:, ds(k)], None, ALU.is_equal)

            def extra_one_hot(base, k, s):
                one_hot(S_x, rel_x, relx_ready, base + k, k, s).then_inc(sx_ready, 1)

            def back_prepare(blocks, s):
                lo, hi, base = blocks
                with dve.If(lo < hi):
                    extra_one_hot(base, lo + 1, s)

            def back(g, blocks, s):
                lo, hi, base = blocks
                dve.wait_ge(agg_done, g + 1)
                nc.vector.tensor_tensor(HU[:, ds(lo * UW, UW)], HU[:, ds(lo * UW, UW)], acc, ALU.add).then_inc(acc_free, 1)
                with dve.If(lo < hi):
                    with dve.Fori(lo + 1, hi + 1) as k:
                        dve.wait_ge(aggx_done, base + k)
                        nc.vector.tensor_tensor(HU[:, ds(k * UW, UW)], HU[:, ds(k * UW, UW)], acc_x, ALU.add).then_inc(addx_done, 1)
                        wait_apart(dve, addx_done, base + k, passed)
                        with dve.If(k < hi):
                            extra_one_hot(base, k + 1, s)

            nc.vector.memset(w1e_sb[:, :], 0.0).then_inc(w_zeroed, 1)
            for t in A:
                nc.vector.memset(t[:, :, D:UW], 1.0).then_inc(a_ones, 1)
            for t in ab_sb:
                nc.vector.memset(t[:, :], 0.0).then_inc(ab_zeroed, 1)
            dve.sem_inc(s_ready, 1)
            dve.sem_inc(h_added, RING)
            dve.sem_inc(acc_free, 1)
            dve.sem_inc(stx_ready, CREDIT)
            dve.sem_inc(relx_ready, CREDIT)
            dve.sem_inc(sx_ready, CREDIT)
            dve.sem_inc(addx_done, CREDIT)
            prepare(0, 1)
            with dve.Fori(0, BODIES) as i:
                blocks = block_range(nc, dve, rng, STEPS * i)
                for s in range(STEPS):
                    g = STEPS * i + s
                    lo, hi, base = blocks
                    dve.wait_ge(bc_ready, g + 1)
                    one_hot_T(ST, lo).then_inc(st_ready, 1)
                    with dve.If(lo < hi):
                        with dve.Fori(lo + 1, hi + 1) as k:
                            dve.wait_ge(hx_done, base + k - 1)
                            one_hot_T(ST_x, k).then_inc(stx_ready, 1)
                    if s % HALF == 0:
                        dve.wait_ge(dst_ready, 2 * i + s // HALF + 1)
                    one_hot(S[s % 2], rel[s % 2], rel_ready, g + 1, lo, s).then_inc(s_ready, 1)
                    if s == 0:
                        with dve.If(i > 0):
                            back_prepare(block_range(nc, dve, rng, g - 1), STEPS - 1)
                    else:
                        back_prepare(before, s - 1)
                    if s < STEPS - 1:
                        following = block_range(nc, dve, rng, g + 1)
                    wait_apart(dve, h_ready, g + 1, passed)
                    with dve.If(lo < hi):
                        wait_apart(dve, hx_done, base + hi, passed)
                    dve.wait_ge(gathered[s % RING], 16 * GROUP * (STEPS // RING * i + s // RING + 1))
                    dve.wait_ge(silu_done, g + 1)
                    nc.vector.tensor_tensor(pre[s % 2][:, :], h_ps[s % 2], G[s % RING][:, :], ALU.add).then_inc(h_added, 1)
                    if s == 0:
                        with dve.If(i > 0):
                            back(g - 1, block_range(nc, dve, rng, g - 1), STEPS - 1)
                    else:
                        back(g - 1, before, s - 1)
                    if s % HALF == 3:
                        m = s // HALF
                        prepare(1 - m, i + 1 + m)
                    before, blocks = blocks, following
            last_blocks = block_range(nc, dve, rng, GROUPS - 1)
            back_prepare(last_blocks, STEPS - 1)
            back(GROUPS - 1, last_blocks, STEPS - 1)

        @block.tensor
        def _(pe):
            pe.sem_inc(ea_used, RING)
            pe.sem_inc(hx_done, CREDIT)
            pe.sem_inc(aggx_done, CREDIT)
            pe.wait_ge(w_loaded, 32)

            def edge_part(s):
                for v in range(GROUP // 2):
                    last = nc.tensor.matmul(h_ps[s % 2][:, 2 * v * P:2 * (v + 1) * P], ea[s % RING][:, v * P:(v + 1) * P],
                                            w1e_sb[:, :], start=(2 * v * P % BANK == 0), stop=False, skip_group_check=True)
                return last

            def dst_part(onehot_T, k, s):
                for u in range(GROUP):
                    last = nc.tensor.matmul(h_ps[s % 2][:, u * P:(u + 1) * P], onehot_T[:, u * P:(u + 1) * P],
                                            Hd[:, ds(k * D, D)], start=False, stop=True, skip_group_check=True)
                return last

            def aggregate(out, onehot, s):
                for u in range(GROUP):
                    last = nc.tensor.matmul(out, onehot[:, u * P:(u + 1) * P], A[s % 2][:, u, :],
                                            start=(u == 0), stop=(u == GROUP - 1))
                return last

            def back(g, blocks, s):
                lo, hi, base = blocks
                pe.wait_ge(silu_done, 2 + g + 1)
                pe.wait_ge(s_ready, 1 + g + 1)
                pe.wait_ge(acc_free, g + 1)
                aggregate(acc, S[s % 2], s).then_inc(agg_done, 1)
                with pe.If(lo < hi):
                    with pe.Fori(lo + 1, hi + 1) as k:
                        pe.wait_ge(sx_ready, base + k)
                        aggregate(acc_x, S_x, s).then_inc(aggx_done, 1)

            with pe.Fori(0, BODIES) as i:
                for s in range(STEPS):
                    g = STEPS * i + s
                    times = STEPS // RING * i + s // RING + 1
                    pe.wait_ge(ab_loaded[s % RING], 16 * times)
                    pe.wait_ge(s_ready, g + 1)
                    for half in range(2):
                        cols = slice(half * GE // 2, (half + 1) * GE // 2)
                        last = nc.tensor.matmul(bc[:, cols], ones2[:, :], ab_sb[s % RING][:, cols], start=True, stop=True)
                    last.then_inc(bc_ready, 1)
                    pe.wait_ge(ea_loaded[s % RING], 16 * times)
                    pe.wait_ge(h_added, g + RING - 1)
                    edge_part(s).then_inc(ea_used, 1)
                    blocks = block_range(nc, pe, rng, g)
                    lo, hi, base = blocks
                    pe.wait_ge(st_ready, g + 1)
                    dst_part(ST, lo, s).then_inc(h_ready, 1)
                    with pe.If(lo < hi):
                        with pe.Fori(lo + 1, hi + 1) as k:
                            pe.wait_ge(stx_ready, base + k)
                            dst_part(ST_x, k, s).then_inc(hx_done, 1)
                    if s == 0:
                        with pe.If(i > 0):
                            back(g - 1, block_range(nc, pe, rng, g - 1), STEPS - 1)
                    else:
                        back(g - 1, before, s - 1)
                    before = blocks
            back(GROUPS - 1, block_range(nc, pe, rng, GROUPS - 1), STEPS - 1)


def phase_update(nc, keep, x1, x1T, w2T, wgt_top, wgt_bot, b2, bgt, gamma, beta, out):
    HU, ps, ident, eps = keep["HU"], keep["ps"], keep["ident"], keep["eps"]
    with ExitStack() as stack:
        b = Build(nc, stack)
        w2T_sb = b.sb("w2T_sb", [P, D])
        top = b.sb("top", [P, 2 * D])
        bot = b.sb("bot", [P, 2 * D])
        b2_sb = b.sb("b2_sb", [P, 1])
        b2_all = b.sb("b2_all", [P, P])
        bgt_sb = b.sb("bgt_sb", [P, 2 * D])
        gamma_sb, beta_sb = b.sb("gamma_sb", [P, D]), b.sb("beta_sb", [P, D])
        w2b = b.sb("w2b", [P, 2 * D])
        b2b = b.sb("b2b", [P, 2 * D])
        x1_sb = [b.sb(f"x1_sb{i}", [P, CH, D]) for i in range(2)]
        x1T_sb = [b.sb(f"ux1T_sb{i}", [P, CH * P]) for i in range(2)]
        V = b.sb("V", [P, CH, D])
        VT = b.sb("VT", [P, CH * P])
        z = b.sb("z", [P, CH, 2 * D])
        y = [b.sb(f"y{i}", [P, CH, D]) for i in range(2)]
        cnt = b.sb("cnt", [P, CH])
        has = b.sb("has", [P, CH])
        stats = b.sb("ustats", [P, CH, 6])
        mv = b.sb("umv", [P, CH, 2])
        sd = b.sb("usd", [P, CH])
        tps = ps[:, 0:CH * P]
        zps = ps[:, 1024:1024 + CH * 2 * D].rearrange("p (j n) -> p j n", j=CH)

        w_loaded = b.sem("uw_loaded")
        folded, fold_out = b.sem("folded"), b.sem("fold_out")
        b2_all_ready = b.sem("b2_all_ready")
        x_loaded = [b.sem(f"ux_loaded{i}") for i in range(2)]
        out_stored = [b.sem(f"out_stored{i}") for i in range(2)]
        v_ready, t_done, vT_ready = b.sem("v_ready"), b.sem("ut_done"), b.sem("vT_ready")
        z_done, z_ready, gates = b.sem("z_done"), b.sem("z_ready"), b.sem("gates")
        chain = b.sem("uchain")
        sd_done = b.sem("usd_done")
        y_done = b.sem("y_done")
        CHAIN = 17
        passed = keep["passed"]
        block = stack.enter_context(nc.Block())

        def rows(dram, c):
            return dram[ds(c * CH * P, CH * P), :].rearrange("(j p) f -> p j f", p=P)

        def over_blocks(row):
            return row[:, :].rearrange("p (o f) -> p o f", o=1).to_broadcast([P, CH, row.shape[-1]])

        def over_cols(col, n):
            return col[:, :].rearrange("p (j o) -> p j o", o=1).to_broadcast([P, CH, n])

        @block.sync
        def _(sp):
            loads = [(w2T_sb[:, :], w2T), (top[:, :], wgt_top), (bot[:, :], wgt_bot), (b2_sb[:, :], b2),
                     (bgt_sb[:, :], bgt.to_broadcast([P, 2 * D])), (gamma_sb[:, :], gamma.to_broadcast([P, D])),
                     (beta_sb[:, :], beta.to_broadcast([P, D]))]
            for to, of in loads:
                sp.dma_start(to, of).then_inc(w_loaded, 16)
            for s in range(2):
                sp.sem_inc(out_stored[s], 16)
            with sp.Fori(0, CHUNKS // 2) as i:
                for s in range(2):
                    c = 2 * i + s
                    sp.wait_ge(y_done, c + 1)
                    sp.dma_start(x1_sb[s][:, :, :], rows(x1, c)).then_inc(x_loaded[s], 16)
                    sp.dma_start(x1T_sb[s][:, :], x1T[:, ds(c * CH * P, CH * P)]).then_inc(x_loaded[s], 16)

        LOADED = 7 * 16

        @block.tensor
        def _(pe):
            pe.wait_ge(w_loaded, LOADED)
            nc.tensor.matmul(ps[:, 0:2 * D], w2T_sb[:, :], bot[:, :], start=True, stop=True).then_inc(folded, 1)
            pe.wait_ge(b2_all_ready, 1)
            nc.tensor.matmul(ps[:, 512:512 + 2 * D], b2_all[:, :], bot[:, :], start=True, stop=True).then_inc(folded, 1)
            pe.wait_ge(fold_out, 2)
            with pe.Fori(0, CHUNKS // 2) as i:
                for s in range(2):
                    c = 2 * i + s
                    pe.wait_ge(v_ready, c + 1)
                    for j in range(CH):
                        last = nc.tensor.transpose(tps[:, j * P:(j + 1) * P], V[:, j, :], ident[:, :])
                    last.then_inc(t_done, 1)
                    pe.wait_ge(x_loaded[s], 32 * (i + 1))
                    pe.wait_ge(vT_ready, c + 1)
                    for j in range(CH):
                        nc.tensor.matmul(zps[:, j, :], x1T_sb[s][:, j * P:(j + 1) * P], top[:, :], start=True, stop=False)
                        last = nc.tensor.matmul(zps[:, j, :], VT[:, j * P:(j + 1) * P], w2b[:, :], start=False, stop=True)
                    last.then_inc(z_done, 1)

        @block.scalar
        def _(act):
            act.wait_ge(folded, 2)
            nc.scalar.activation(w2b[:, :], ps[:, 0:2 * D], ACT.Copy).then_inc(fold_out, 1)
            nc.scalar.activation(b2b[:, :], ps[:, 512:512 + 2 * D], ACT.Copy).then_inc(fold_out, 1)
            with act.Fori(0, CHUNKS // 2) as i:
                for s in range(2):
                    c = 2 * i + s
                    act.wait_ge(t_done, c + 1)
                    nc.scalar.activation(VT[:, :], tps, ACT.Copy).then_inc(vT_ready, 1)
                    act.wait_ge(z_ready, c + 1)
                    nc.scalar.activation(z[:, :, 0:D], z[:, :, 0:D], ACT.Sigmoid).then_inc(gates, 1)
                    nc.scalar.activation(z[:, :, D:2 * D], z[:, :, D:2 * D], ACT.Tanh).then_inc(gates, 1)
                    for n in range(2):
                        act.wait_ge(chain, CHAIN * c + (9, 16)[n])
                        nc.scalar.activation(sd[:, :], mv[:, :, 1], ACT.Sqrt, bias=eps[:, :]).then_inc(sd_done, 1)
                    act.wait_ge(y_done, 2 + c + 1)
                    act.dma_start(rows(out, c), y[s][:, :, :]).then_inc(out_stored[s], 16)
            for s in range(2):
                act.wait_ge(out_stored[s], 16 * (CHUNKS // 2 + 1))

        @block.vector
        def _(dve):
            dve.sem_inc(y_done, 2)
            dve.wait_ge(w_loaded, LOADED)
            nc.vector.tensor_copy(b2_all[:, :], b2_sb[:, :].to_broadcast([P, P])).then_inc(b2_all_ready, 1)
            dve.wait_ge(fold_out, 2)
            with dve.Fori(0, CHUNKS // 2) as i:
                for s in range(2):
                    c = 2 * i + s
                    done = [CHAIN * c]

                    def then(ins):
                        ins.then_inc(chain, 1)
                        done[0] = done[0] + 1
                        dve.wait_ge(chain, done[0])

                    def normalise(src, dst_t, n):
                        layer_norm_stats(nc, dve, src, stats, mv, chain, done[0], passed)
                        done[0] = done[0] + 2
                        dve.wait_ge(sd_done, 2 * c + n + 1)
                        then(nc.vector.reciprocal(sd[:, :], sd[:, :]))
                        for j in range(CH):
                            last = nc.vector.tensor_scalar(dst_t[:, j, :], src[:, j, :], mv[:, j, 0:1], sd[:, j:j + 1],
                                                           ALU.subtract, ALU.mult)
                        return last

                    hu = HU[:, ds(c * CH * UW, CH * UW)].rearrange("p (j n) -> p j n", j=CH)
                    nc.vector.tensor_scalar(has[:, :], hu[:, :, D], 1.0, None, ALU.min)
                    then(nc.vector.tensor_scalar(cnt[:, :], hu[:, :, D], 1.0, None, ALU.max))
                    then(nc.vector.reciprocal(cnt[:, :], cnt[:, :]))
                    nc.vector.tensor_tensor(V[:, :, :], hu[:, :, 0:D], over_cols(cnt, D), ALU.mult).then_inc(v_ready, 1)
                    then(nc.vector.tensor_tensor(z[:, :, :], over_blocks(b2b), over_cols(has, 2 * D), ALU.mult))
                    then(nc.vector.tensor_tensor(z[:, :, :], z[:, :, :], over_blocks(bgt_sb), ALU.add))
                    dve.wait_ge(z_done, c + 1)
                    nc.vector.tensor_tensor(z[:, :, :], z[:, :, :], zps, ALU.add).then_inc(z_ready, 1)
                    dve.wait_ge(gates, 2 * c + 2)
                    dve.wait_ge(x_loaded[s], 32 * (i + 1))
                    dve.wait_ge(out_stored[s], 16 * (i + 1))
                    gate, tr, x1c, yc = z[:, :, 0:D], z[:, :, D:2 * D], x1_sb[s][:, :, :], y[s][:, :, :]
                    then(nc.vector.tensor_tensor(yc, x1c, tr, ALU.subtract))
                    then(nc.vector.tensor_tensor(yc, yc, gate, ALU.mult))
                    then(nc.vector.tensor_tensor(yc, yc, tr, ALU.add))
                    then(normalise(y[s], y[s], 0))
                    then(nc.vector.tensor_tensor(yc, yc, over_blocks(gamma_sb), ALU.mult))
                    then(nc.vector.tensor_tensor(x1c, x1c, over_blocks(beta_sb), ALU.add))
                    then(nc.vector.tensor_tensor(yc, yc, x1c, ALU.add))
                    normalise(y[s], y[s], 1).then_inc(y_done, 1)


def build_program(nc, x, xT, meta, wts, dst_tiles, dst_rows, edges, w0, w1sd, w1e, b1, w2T, b2, wgt_top, wgt_bot,
                  bgt, gamma, beta, out):
    hr = nc.dram_tensor("hr", (NPAD * NREL, D), F32).ap()
    hs = nc.dram_tensor("hs", (NPAD, D), F32).ap()
    x1 = nc.dram_tensor("x1", (NPAD, D), F32).ap()
    x1T = nc.dram_tensor("x1T", (D, NPAD), F32).ap()
    ab = nc.dram_tensor("ab", (2, EPAD), BF16).ap()
    with ExitStack() as stack:
        b = Build(nc, stack)
        keep = {
            "rng": b.sb("rng", [1, GROUPS + 1], I32),
            "HU": b.sb("HU", [P, BLOCKS * UW]),
            "iota_row": b.sb("iota_row", [P, P]),
            "neg_kb": b.sb("neg_kb", [P, BLOCKS + 1]),
            "node_id": b.sb("node_id", [P, BLOCKS]),
            "pid_i": b.sb("pid_i", [P, BLOCKS], I32),
            "ones2": b.sb("ones2", [P, P], BF16),
            "ident": b.sb("ident", [P, P]),
            "eps": b.sb("eps", [P, 1]),
            "dst_ready0": b.sem("dst_ready"),
            "passed": b.sem("passed"),
            "ps": stack.enter_context(nc.psum_tensor("ps", [P, 4096], F32)),
        }
        phase_tables(nc, keep, xT, w0, dst_tiles, dst_rows, hr, ab)
        phase_relational(nc, keep, meta, wts, hr)
        keep["Hd"] = b.sb("Hd", [P, BLOCKS * D])
        phase_nodes(nc, keep, x, w1sd, b1, x1, x1T, hs)
        phase_messages(nc, keep, meta, edges, ab, w1e, hs)
        phase_update(nc, keep, x1, x1T, w2T, wgt_top, wgt_bot, b2, bgt, gamma, beta, out)


def kernel(x, src, dst, edge_attr_64, edge_type_3, edge_weight, L0_gnn_weight, L1_gnn_W1, L1_gnn_b1, L1_gnn_W2,
           L1_gnn_b2, L1_gnn_Wg, L1_gnn_bg, L1_gnn_Wt, L1_gnn_bt, L1_gnn_gamma, L1_gnn_beta):
    import numpy as np
    from concourse import bacc
    from concourse.bass_utils import run_bass_kernel_spmd

    def padded(a, n, value=0):
        a = np.asarray(a)
        return np.concatenate([a, np.full((n - a.shape[0], *a.shape[1:]), value, a.dtype)])

    def by_half(a):
        return a.reshape(-1, HC, P).transpose(0, 2, 1)

    more = EPAD + HC * P
    src_p, typ_p = padded(src, more), padded(edge_type_3, more)
    dst_p = padded(dst, more, NPAD - 1)
    x_p = padded(x, NPAD)
    arrays = {
        "x": x_p,
        "xT": x_p.T,
        "meta": np.stack([by_half(src_p), by_half(typ_p), by_half(dst_p)], axis=2),
        "wts": by_half(padded(edge_weight, more)),
        "dst_tiles": dst_p[:EPAD].reshape(TILES, P).T,
        "dst_rows": dst_p[:EPAD].reshape(P, TILES),
        "edges": padded(edge_attr_64, EPAD).reshape(GROUPS, GROUP // 2, 2, P, DE).transpose(0, 2, 4, 1, 3).reshape(GROUPS, P, GE // 2),
        "w0": np.asarray(L0_gnn_weight).transpose(1, 0, 2).reshape(D, NREL * D),
        "w1sd": np.concatenate([np.asarray(L1_gnn_W1)[0:D], np.asarray(L1_gnn_W1)[D:2 * D]], axis=1),
        "w1e": np.asarray(L1_gnn_W1)[2 * D:],
        "b1": np.asarray(L1_gnn_b1).reshape(1, D),
        "w2T": np.asarray(L1_gnn_W2).T,
        "b2": np.asarray(L1_gnn_b2).reshape(D, 1),
        "wgt_top": np.concatenate([np.asarray(L1_gnn_Wg)[0:D], np.asarray(L1_gnn_Wt)[0:D]], axis=1),
        "wgt_bot": np.concatenate([np.asarray(L1_gnn_Wg)[D:], np.asarray(L1_gnn_Wt)[D:]], axis=1),
        "bgt": np.concatenate([np.asarray(L1_gnn_bg), np.asarray(L1_gnn_bt)]).reshape(1, 2 * D),
        "gamma": np.asarray(L1_gnn_gamma).reshape(1, D),
        "beta": np.asarray(L1_gnn_beta).reshape(1, D),
    }
    arrays = {name: np.ascontiguousarray(a) for name, a in arrays.items()}
    nc = bacc.Bacc("TRN2", target_bir_lowering=False, num_devices=1)
    args = [nc.dram_tensor(f"in_{n}", a.shape, mybir.dt.from_np(a.dtype), kind="ExternalInput").ap() for n, a in arrays.items()]
    out = nc.dram_tensor("out_0", (NPAD, D), F32, kind="ExternalOutput").ap()
    build_program(nc, *args, out)
    r = run_bass_kernel_spmd(nc, [{f"in_{n}": a for n, a in arrays.items()}], core_ids=[0])
    return r.results[0]["out_0"][:NODES]
```

```python
from contextlib import ExitStack

import concourse.bass as bass
from concourse import mybir

ALU = mybir.AluOpType
ACT = mybir.ActivationFunctionType
AX = mybir.AxisListType
F32 = mybir.dt.float32
I32 = mybir.dt.int32
BF16 = mybir.dt.bfloat16
RMAX = bass.bass_isa.ReduceOp.max

P = 128
NODES = 12500
EDGES = 400000
D = 128
DE = 64
NREL = 3
EPS = 1e-5
BLOCKS = -(-NODES // P)
NPAD = BLOCKS * P
GROUP = 8
GE = GROUP * P
STEPS = 8
HALF = 4
HC = HALF * GROUP
GROUPS = -(-EDGES // (GE * STEPS)) * STEPS
BODIES = GROUPS // STEPS
HALVES = GROUPS // HALF
EPAD = GROUPS * GE
TILES = EPAD // P
RING = 4
CH = 7
CHUNKS = BLOCKS // CH
UW = D + 1
BANK = 512
CREDIT = P


def ds(i, n=1):
    return bass.ds(i, n)


def wait_apart(eng, sem, value, passed):
    eng.wait_ge(sem, value)
    eng.sem_inc(passed, 1)


class Build:

    def __init__(self, nc, stack):
        self.nc, self.stack = nc, stack

    def sb(self, name, shape, dt=F32):
        return self.stack.enter_context(self.nc.sbuf_tensor(name, shape, dt))

    def sem(self, name):
        return self.stack.enter_context(self.nc.semaphore(name))


def block_range(nc, eng, rng, g):
    word = eng.value_load(rng[0:1, ds(g + 1)], min_val=0, max_val=2 ** 31 - 1)
    why = "phase_tables clamps blocks to those there are, and their number bounds the count"
    return tuple(nc.s_assert_within(eng.snap(v), 0, most, skip_runtime_bounds_check_because=why)
                 for v, most in ((word % P, BLOCKS - 1), (word // P % P, BLOCKS - 1),
                                 (word // (P * P), GROUPS * BLOCKS + CREDIT)))


def phase_tables(nc, keep, xT, w0, dst_tiles, hr):
    rng, HU = keep["rng"], keep["HU"]
    iota_row, neg_kb, node_id, ones2 = keep["iota_row"], keep["neg_kb"], keep["node_id"], keep["ones2"]
    ps = keep["ps"]
    with ExitStack() as stack:
        b = Build(nc, stack)
        w0_sb = b.sb("w0_sb", [P, NREL * D])
        xT_sb = [b.sb(f"xT_sb{i}", [P, CH * P]) for i in range(2)]
        stage = [b.sb(f"hr_stage{i}", [P, CH, NREL * D]) for i in range(2)]
        dst_i = b.sb("dst_i", [P, TILES], I32)
        ext = b.sb("ext", [P, 2, GROUPS])
        ext_all = b.sb("ext_all", [P, 2, GROUPS])
        lohi_i = b.sb("lohi_i", [1, 2, GROUPS], I32)
        lohi = b.sb("lohi", [1, 2, GROUPS])
        one_row = b.sb("one_row", [1, GROUPS])
        extras = b.sb("extras", [1, GROUPS])
        low_bits, high_bits = b.sb("low_bits", [1, GROUPS], I32), b.sb("high_bits", [1, GROUPS], I32)
        upto = b.sb("upto", [1, GROUPS])
        kb_i = b.sb("kb_i", [P, BLOCKS + 1], I32)
        io_i = b.sb("io_i", [P, P], I32)

        w0_loaded = b.sem("w0_loaded")
        dst_loaded = b.sem("dst_loaded")
        xT_loaded = [b.sem(f"xT_loaded{i}") for i in range(2)]
        hr_stored = [b.sem(f"hr_stored{i}") for i in range(2)]
        mm_done = b.sem("mm_done")
        act_out = b.sem("act_out")
        dve_out = b.sem("dve_out")
        v_chain = b.sem("v_chain")
        ext_ready, ext_reduced = b.sem("ext_ready"), b.sem("ext_reduced")
        iotas = b.sem("iotas")
        EV, OD = (CH + 1) // 2, CH // 2
        passed = keep["passed"]
        block = stack.enter_context(nc.Block())

        @block.sync
        def _(sp):
            sp.dma_start(w0_sb[:, :], w0).then_inc(w0_loaded, 16)
            with sp.Fori(0, CHUNKS // 2) as i:
                for s in range(2):
                    sp.wait_ge(mm_done, CH * (2 * i + s + 1))
                    sp.dma_start(xT_sb[s][:, :], xT[:, ds((2 * i + s) * CH * P, CH * P)]).then_inc(xT_loaded[s], 16)
                with sp.If(i == 0):
                    sp.dma_start(dst_i[:, :], dst_tiles).then_inc(dst_loaded, 16)

        @block.gpsimd
        def _(pool):
            nc.gpsimd.iota(kb_i[:, :], pattern=[[-P, BLOCKS + 1]], base=0, channel_multiplier=0).then_inc(iotas, 1)
            nc.gpsimd.iota(io_i[:, :], pattern=[[1, P]], base=0, channel_multiplier=0).then_inc(iotas, 1)
            nc.gpsimd.memset(ones2[:, :], 1.0)
            nc.gpsimd.memset(keep["ident"][:, :], 0.0).then_inc(iotas, 1)
            pool.wait_ge(iotas, 3)
            nc.gpsimd.affine_select(out=keep["ident"][:, :], in_=keep["ident"][:, :], compare_op=ALU.not_equal,
                                    fill=1.0, base=0, pattern=[[-1, P]], channel_multiplier=1).then_inc(iotas, 1)
            nc.gpsimd.iota(keep["pid_i"][:, :], pattern=[[P, BLOCKS]], base=0, channel_multiplier=1).then_inc(iotas, 1)
            pool.wait_ge(ext_ready, 1)
            nc.gpsimd.partition_all_reduce(ext_all[:, :, :].rearrange("p a g -> p (a g)"),
                                           ext[:, :, :].rearrange("p a g -> p (a g)"), P, RMAX).then_inc(ext_reduced, 1)
            nc.gpsimd.memset(HU[:, :], 0.0)

        @block.tensor
        def _(pe):
            pe.sem_inc(mm_done, 2 * CH)
            pe.wait_ge(w0_loaded, 16)
            with pe.Fori(0, CHUNKS // 2) as i:
                for s in range(2):
                    c = 2 * i + s
                    pe.wait_ge(xT_loaded[s], 16 * (i + 1))
                    for j in range(CH):
                        if j % 2 == 0:
                            pe.wait_ge(act_out, EV * c + j // 2 + 1)
                        else:
                            pe.wait_ge(dve_out, OD * c + j // 2 + 1)
                        nc.tensor.matmul(ps[:, 512 * j:512 * j + NREL * D], xT_sb[s][:, j * P:(j + 1) * P],
                                         w0_sb[:, :], start=True, stop=True).then_inc(mm_done, 1)

        @block.scalar
        def _(act):
            act.sem_inc(act_out, EV)
            with act.Fori(0, CHUNKS // 2) as i:
                for s in range(2):
                    c = 2 * i + s
                    act.wait_ge(hr_stored[s], 16 * (i + 1))
                    for j in range(0, CH, 2):
                        act.wait_ge(mm_done, 2 * CH + CH * c + j + 1)
                        nc.scalar.activation(stage[s][:, j, :], ps[:, 512 * j:512 * j + NREL * D],
                                             ACT.Copy).then_inc(act_out, 1)
                    act.wait_ge(act_out, EV * (c + 2))
                    act.wait_ge(dve_out, OD * (c + 2))
                    act.dma_start(hr[ds(c * CH * P * NREL, CH * P * NREL), :].rearrange("(p j r) f -> p j (r f)", p=P, r=NREL),
                                  stage[s][:, :, :]).then_inc(hr_stored[s], 16)
            for s in range(2):
                act.wait_ge(hr_stored[s], 16 * (CHUNKS // 2 + 1))

        @block.vector
        def _(dve):
            def extremes():
                dve.wait_ge(dst_loaded, 16)
                groups = dst_i[:, :].rearrange("p (g u) -> p g u", u=GROUP)
                nc.vector.tensor_reduce(ext[:, 0, :], groups, axis=AX.X, op=ALU.max)
                nc.vector.tensor_reduce(ext[:, 1, :], groups, axis=AX.X, op=ALU.min).then_inc(v_chain, 1)
                dve.wait_ge(v_chain, 1)
                nc.vector.tensor_scalar(ext[:, 1, :], ext[:, 1, :], -1.0, None, ALU.mult).then_inc(ext_ready, 1)

            def ranges():
                dve.wait_ge(ext_reduced, 1)
                nc.vector.tensor_copy(lohi_i[0:1, 0, :], ext_all[0:1, 0, :])
                nc.vector.tensor_scalar(lohi_i[0:1, 1, :], ext_all[0:1, 1, :], -1.0, None, ALU.mult).then_inc(v_chain, 1)
                nc.vector.memset(one_row[:, :], 1.0).then_inc(v_chain, 1)
                dve.wait_ge(v_chain, 3)
                nc.vector.tensor_scalar(lohi_i[:, :, :], lohi_i[:, :, :], 7, None, ALU.arith_shift_right).then_inc(v_chain, 1)
                dve.wait_ge(v_chain, 4)
                nc.vector.tensor_scalar(lohi[:, :, :], lohi_i[:, :, :], 0.0, float(BLOCKS - 1), ALU.max, ALU.min).then_inc(v_chain, 1)
                dve.wait_ge(v_chain, 5)
                nc.vector.scalar_tensor_tensor(out=low_bits[:, :], in0=lohi[:, 0, :], scalar=float(P), in1=lohi[:, 1, :],
                                               op0=ALU.mult, op1=ALU.add)
                nc.vector.tensor_tensor(extras[:, :], lohi[:, 0, :], lohi[:, 1, :], ALU.subtract).then_inc(v_chain, 1)
                dve.wait_ge(v_chain, 6)
                nc.vector.tensor_tensor_scan(upto[:, :], one_row[:, :], extras[:, :], 0.0, ALU.mult, ALU.add).then_inc(v_chain, 1)
                dve.wait_ge(v_chain, 7)
                nc.vector.scalar_tensor_tensor(out=high_bits[:, :], in0=upto[:, :], scalar=float(CREDIT), in1=lohi[:, 0, :],
                                               op0=ALU.add, op1=ALU.subtract).then_inc(v_chain, 1)
                dve.wait_ge(v_chain, 8)
                nc.vector.tensor_scalar(high_bits[:, :], high_bits[:, :], 14, None, ALU.arith_shift_left).then_inc(v_chain, 1)
                dve.wait_ge(v_chain, 9)
                nc.vector.tensor_tensor(rng[0:1, 1:], high_bits[:, :], low_bits[:, :], ALU.bitwise_or)

            dve.sem_inc(dve_out, OD)
            for s in range(2):
                dve.sem_inc(hr_stored[s], 16)
            dve.wait_ge(iotas, 5)
            nc.vector.tensor_copy(neg_kb[:, :], kb_i[:, :])
            nc.vector.tensor_copy(iota_row[:, :], io_i[:, :])
            nc.vector.tensor_copy(node_id[:, :], keep["pid_i"][:, :])
            nc.vector.memset(keep["eps"][:, :], EPS)
            with dve.Fori(0, CHUNKS // 2) as i:
                for s in range(2):
                    c = 2 * i + s
                    dve.wait_ge(hr_stored[s], 16 * (i + 1))
                    for j in range(1, CH, 2):
                        dve.wait_ge(mm_done, 2 * CH + CH * c + j + 1)
                        nc.vector.tensor_copy(stage[s][:, j, :], ps[:, 512 * j:512 * j + NREL * D]).then_inc(dve_out, 1)
                with dve.If(i == 1):
                    extremes()
                with dve.If(i == CHUNKS // 4):
                    ranges()


def phase_relational(nc, keep, meta, wts, hr, dst_rows, ab, update_weights):
    w2T, wgt_top, wgt_bot, b2, bgt, gamma, beta = update_weights
    rng, HU, iota_row, neg_kb, ps = keep["rng"], keep["HU"], keep["iota_row"], keep["neg_kb"], keep["ps"]
    with ExitStack() as stack:
        b = Build(nc, stack)
        meta_sb = [b.sb(f"meta_sb{i}", [P, 3, HC], I32) for i in range(2)]
        w_sb = [b.sb(f"w_sb{i}", [P, HC]) for i in range(2)]
        idx = [b.sb(f"idx{i}", [P, HC], I32) for i in range(2)]
        dstf = [b.sb(f"dstf{i}", [P, HC]) for i in range(2)]
        rel = [b.sb(f"rel{i}", [P, GROUP]) for i in range(2)]
        rel_x = b.sb("rel_x", [P, GROUP])
        S = [b.sb(f"S{i}", [P, GE]) for i in range(2)]
        S_x = b.sb("S_x", [P, GE])
        G = [b.sb(f"G{i}", [P, GE]) for i in range(RING)]
        acc, acc_x = ps[:, 0:D], ps[:, 512:512 + D]
        dst_r = b.sb("dst_r", [P, TILES], I32)
        low_i = b.sb("low_i", [P, TILES], I32)
        ab_sb = b.sb("ab_sb", [P, 2, TILES], BF16)
        w2T_sb = b.sb("w2T_sb", [P, D])
        bot = b.sb("bot", [P, 2 * D])
        b2_sb = b.sb("b2_sb", [P, 1])
        b2_all = b.sb("b2_all", [P, P])
        fold_ps = ps[:, 2 * BANK:2 * BANK + 4 * D]
        loads = [(w2T_sb[:, :], w2T), (keep["top"][:, :], wgt_top), (bot[:, :], wgt_bot), (b2_sb[:, :], b2),
                 (keep["bgt"][:, :], bgt.to_broadcast([P, 2 * D])), (keep["gamma"][:, :], gamma.to_broadcast([P, D])),
                 (keep["beta"][:, :], beta.to_broadcast([P, D]))]

        weights_loaded, b2_all_ready, folded = b.sem("weights_loaded"), b.sem("b2_all_ready"), b.sem("folded")
        rows_loaded, ab_stored = b.sem("rows_loaded"), b.sem("ab_stored")
        low_ready, ab_ready = b.sem("low_ready"), b.sem("ab_ready")

        meta_loaded = [b.sem(f"meta_loaded{i}") for i in range(2)]
        w_loaded = [b.sem(f"w_loaded{i}") for i in range(2)]
        idx_ready = b.sem("idx_ready")
        dst_ready = b.sem("dst_ready")
        gathered = [b.sem(f"gathered{i}") for i in range(RING)]
        s_ready, agg_done = b.sem("s_ready"), b.sem("agg_done")
        acc_free = b.sem("acc_free")
        sx_ready, aggx_done = b.sem("sx_ready"), b.sem("aggx_done")
        rel_ready, relx_ready = b.sem("rel_ready"), b.sem("relx_ready")
        addx_done = b.sem("addx_done")
        step_done = b.sem("step_done")
        passed = keep["passed"]
        block = stack.enter_context(nc.Block())

        @block.gpsimd
        def _(pool):
            def gather(s):
                for u in range(GROUP):
                    col = (s % HALF) * GROUP + u
                    nc.gpsimd.indirect_dma_start(
                        out=G[s % RING][:, u * P:(u + 1) * P], out_offset=None, in_=hr,
                        in_offset=bass.IndirectOffsetOnAxis(ap=idx[s // HALF][:, col:col + 1], axis=0),
                    ).then_inc(gathered[s % RING], 16)

            with pool.Fori(0, BODIES) as i:
                for s in range(STEPS):
                    g = STEPS * i + s
                    if s % HALF == 0:
                        pool.wait_ge(idx_ready, 2 * i + s // HALF + 1)
                    wait_apart(pool, step_done, g + 3, passed)
                    gather(s)

        @block.sync
        def _(sp):
            sp.dma_start(dst_r[:, :], dst_rows).then_inc(rows_loaded, 16)
            for to, of in loads:
                sp.dma_start(to, of).then_inc(weights_loaded, 16)
            sp.wait_ge(ab_ready, 1)
            sp.dma_start(ab.rearrange("a (p n) -> p a n", p=P), ab_sb[:, :, :]).then_inc(ab_stored, 16)
            sp.wait_ge(ab_stored, 16)

        @block.scalar
        def _(act):
            def load(h, m):
                act.dma_start(meta_sb[m][:, :, :], meta[ds(h), :, :, :].rearrange("o p a c -> (o p) a c")).then_inc(meta_loaded[m], 16)
                act.dma_start(w_sb[m][:, :], wts[ds(h), :, :].rearrange("o p c -> (o p) c")).then_inc(w_loaded[m], 16)

            load(0, 0)
            act.wait_ge(folded, 2)
            nc.scalar.activation(keep["w2b"][:, :], fold_ps[:, 0:2 * D], ACT.Copy)
            nc.scalar.activation(keep["b2b"][:, :], fold_ps[:, 2 * D:4 * D], ACT.Copy)
            with act.Fori(0, BODIES) as i:
                for m in range(2):
                    act.wait_ge(step_done, RING + 1 + STEPS * i + HALF * m + 1)
                    load(2 * i + m + 1, 1 - m)

        @block.vector
        def _(dve):
            def prepare(h, m, times):
                dve.wait_ge(meta_loaded[m], 16 * times)
                dve.wait_ge(w_loaded[m], 16 * times)
                nc.vector.scalar_tensor_tensor(out=idx[m][:, :], in0=meta_sb[m][:, 0, :], scalar=float(NREL),
                                               in1=meta_sb[m][:, 1, :], op0=ALU.mult, op1=ALU.add).then_inc(idx_ready, 1)
                nc.vector.tensor_copy(dstf[m][:, :], meta_sb[m][:, 2, :]).then_inc(dst_ready, 1)

            def one_hot(out, rel_t, ready, count, k, s):
                m, c0 = s // HALF, (s % HALF) * GROUP
                nc.vector.tensor_scalar(rel_t[:, :], dstf[m][:, c0:c0 + GROUP], neg_kb[:, ds(k)], None,
                                        ALU.add).then_inc(ready, 1)
                dve.wait_ge(ready, count)
                for u in range(GROUP):
                    last = nc.vector.tensor_scalar(out[:, u * P:(u + 1) * P], iota_row[:, :], rel_t[:, u:u + 1],
                                                   w_sb[m][:, c0 + u:c0 + u + 1], ALU.is_equal, ALU.mult)
                return last

            def back(g, s):
                lo, hi, base = block_range(nc, dve, rng, g)
                dve.wait_ge(agg_done, g + 1)
                nc.vector.tensor_tensor(HU[:, ds(lo * UW, D)], HU[:, ds(lo * UW, D)], acc, ALU.add).then_inc(acc_free, 1)
                with dve.If(lo < hi):
                    with dve.Fori(lo + 1, hi + 1) as k:
                        one_hot(S_x, rel_x, relx_ready, base + k, k, s).then_inc(sx_ready, 1)
                        dve.wait_ge(aggx_done, base + k)
                        nc.vector.tensor_tensor(HU[:, ds(k * UW, D)], HU[:, ds(k * UW, D)], acc_x, ALU.add).then_inc(addx_done, 1)
                        wait_apart(dve, addx_done, base + k, passed)

            dve.sem_inc(acc_free, 1)
            dve.sem_inc(relx_ready, CREDIT)
            dve.sem_inc(sx_ready, CREDIT)
            dve.sem_inc(addx_done, CREDIT)
            dve.sem_inc(step_done, RING + 1)
            prepare(0, 0, 1)
            dve.wait_ge(weights_loaded, 16 * len(loads))
            nc.vector.tensor_copy(b2_all[:, :], b2_sb[:, :].to_broadcast([P, P])).then_inc(b2_all_ready, 1)
            dve.wait_ge(rows_loaded, 16)
            nc.vector.tensor_scalar(low_i[:, :], dst_r[:, :], P - 1, None, ALU.bitwise_and).then_inc(low_ready, 1)
            dve.wait_ge(low_ready, 1)
            nc.vector.tensor_tensor(ab_sb[:, 0, :], dst_r[:, :], low_i[:, :], ALU.subtract)
            nc.vector.tensor_copy(ab_sb[:, 1, :], low_i[:, :]).then_inc(ab_ready, 1)
            with dve.Fori(0, BODIES) as i:
                for s in range(STEPS):
                    g = STEPS * i + s
                    if s % HALF == 0:
                        dve.wait_ge(dst_ready, 2 * i + s // HALF + 1)
                    lo, hi, base = block_range(nc, dve, rng, g)
                    one_hot(S[s % 2], rel[s % 2], rel_ready, g + 1, lo, s).then_inc(s_ready, 1)
                    if s == 0:
                        with dve.If(i > 0):
                            back(g - 1, STEPS - 1)
                    else:
                        back(g - 1, s - 1)
                    if s % HALF == 2:
                        m = s // HALF
                        prepare(None, 1 - m, i + 1 + m)
                    dve.drain().then_inc(step_done, 1)
            back(GROUPS - 1, STEPS - 1)

        @block.tensor
        def _(pe):
            pe.sem_inc(aggx_done, CREDIT)
            pe.wait_ge(weights_loaded, 16 * len(loads))
            nc.tensor.matmul(fold_ps[:, 0:2 * D], w2T_sb[:, :], bot[:, :], start=True, stop=True).then_inc(folded, 1)
            pe.wait_ge(b2_all_ready, 1)
            nc.tensor.matmul(fold_ps[:, 2 * D:4 * D], b2_all[:, :], bot[:, :], start=True, stop=True).then_inc(folded, 1)

            def aggregate(out, onehot, s):
                for u in range(GROUP):
                    last = nc.tensor.matmul(out, onehot[:, u * P:(u + 1) * P], G[s % RING][:, u * P:(u + 1) * P],
                                            start=(u == 0), stop=(u == GROUP - 1))
                return last

            with pe.Fori(0, BODIES) as i:
                for s in range(STEPS):
                    g = STEPS * i + s
                    lo, hi, base = block_range(nc, pe, rng, g)
                    pe.wait_ge(s_ready, g + 1)
                    pe.wait_ge(gathered[s % RING], 16 * GROUP * (STEPS // RING * i + s // RING + 1))
                    pe.wait_ge(acc_free, g + 1)
                    aggregate(acc, S[s % 2], s).then_inc(agg_done, 1)
                    with pe.If(lo < hi):
                        with pe.Fori(lo + 1, hi + 1) as k:
                            pe.wait_ge(sx_ready, base + k)
                            aggregate(acc_x, S_x, s).then_inc(aggx_done, 1)


def layer_norm_stats(nc, eng, src, stats, mv, step, n0, ready, passed):
    for j in range(CH):
        last = nc.vector.bn_stats(stats[:, j, :], src[:, j, :])
    last.then_inc(step, 1)
    wait_apart(eng, step, n0 + 1, passed)
    for j in range(CH):
        last = nc.vector.bn_aggr(mv[:, j, :], stats[:, j, :])
    last.then_inc(ready, 1)


def chunk(nc, eng, c):
    return nc.s_assert_within(eng.snap((c + P) % P), 0, CHUNKS - 1, skip_runtime_bounds_check_because="the condition around it")


def stepper(eng, sem, start):
    done = [start]

    def then(ins):
        ins.then_inc(sem, 1)
        done[0] = done[0] + 1
        eng.wait_ge(sem, done[0])
    return then


def phase_nodes(nc, keep, x, w1sd, b1, x1, x1T, hs):
    HU, Hd, ps, ident, eps = keep["HU"], keep["Hd"], keep["ps"], keep["ident"], keep["eps"]
    with ExitStack() as stack:
        b = Build(nc, stack)
        w_sb = b.sb("w1sd_sb", [P, 2 * D])
        b1_sb = b.sb("b1_sb", [P, D])
        x_in = [b.sb(f"x_in{i}", [P, CH, D]) for i in range(2)]
        x_sum = [b.sb(f"x_sum{i}", [P, CH, D]) for i in range(2)]
        x1_sb = [b.sb(f"nx1_sb{i}", [P, CH, D]) for i in range(2)]
        x1T_sb = [b.sb(f"x1T_sb{i}", [P, CH * P]) for i in range(2)]
        hs_sb = [b.sb(f"hs_sb{i}", [P, CH, D]) for i in range(2)]
        mv = [b.sb(f"mv{i}", [P, CH, 2]) for i in range(2)]
        sd = [b.sb(f"sd{i}", [P, CH]) for i in range(2)]
        stats = b.sb("stats", [P, CH, 6])
        zeros = b.sb("zeros", [P, CH * UW])
        tps = ps[:, 0:CH * P]
        hs_ps = ps[:, 1024:1024 + CH * D].rearrange("p (j n) -> p j n", j=CH)
        hd_ps = ps[:, 2048:2048 + CH * D].rearrange("p (j n) -> p j n", j=CH)

        w_loaded = b.sem("w1_loaded")
        x_loaded = [b.sem(f"x_loaded{i}") for i in range(2)]
        x1_stored = [b.sem(f"x1_stored{i}") for i in range(2)]
        x1T_stored = [b.sem(f"x1T_stored{i}") for i in range(2)]
        hs_stored = [b.sem(f"hs_stored{i}") for i in range(2)]
        summed = b.sem("summed")
        stats_ready = b.sem("stats_ready")
        sd_ready = b.sem("sd_ready")
        scaled = b.sem("scaled")
        x1_ready = b.sem("x1_ready")
        t_done, xT_ready = b.sem("t_done"), b.sem("xT_ready")
        h_done = b.sem("h_done")
        hs_ready, hd_done = b.sem("hs_ready"), b.sem("hd_done")
        zeroed = b.sem("zeroed")
        passed = keep["passed"]
        block = stack.enter_context(nc.Block())

        def rows(dram, c):
            return dram[ds(c * CH * P, CH * P), :].rearrange("(j p) f -> p j f", p=P)

        @block.sync
        def _(sp):
            sp.dma_start(w_sb[:, :], w1sd).then_inc(w_loaded, 16)
            sp.dma_start(b1_sb[:, :], b1.to_broadcast([P, D])).then_inc(w_loaded, 16)
            for s in range(2):
                sp.sem_inc(x1_stored[s], 16)
                sp.sem_inc(x1T_stored[s], 16)
                sp.sem_inc(hs_stored[s], 16)
            with sp.Fori(0, CHUNKS // 2) as i:
                for s in range(2):
                    wait_apart(sp, summed, 2 * (2 * i + s) + 1, passed)
                    sp.dma_start(x_in[s][:, :, :], rows(x, 2 * i + s)).then_inc(x_loaded[s], 16)

        @block.gpsimd
        def _(pool):
            nc.gpsimd.memset(zeros[:, :], 0.0).then_inc(zeroed, 1)
            pool.wait_ge(zeroed, 1)
            with pool.Fori(0, CHUNKS // 2) as i:
                for s in range(2):
                    c = 2 * i + s
                    pool.wait_ge(summed, 4 + 2 * c + 1)
                    nc.gpsimd.tensor_copy(HU[:, ds(c * CH * UW, CH * UW)], zeros[:, :]).then_inc(zeroed, 1)

        @block.vector
        def _(dve):
            def project(c):
                dve.wait_ge(h_done, c + 1)
                hd = Hd[:, ds(c * CH * D, CH * D)].rearrange("p (j n) -> p j n", j=CH)
                bias = b1_sb[:, :].rearrange("p (o f) -> p o f", o=1).to_broadcast([P, CH, D])
                nc.vector.tensor_tensor(hd, hd_ps, bias, ALU.add).then_inc(hd_done, 1)

            def normalise(c, s, times):
                dve.wait_ge(sd_ready, c + 1)
                nc.vector.reciprocal(sd[s][:, :], sd[s][:, :]).then_inc(scaled, 1)
                dve.wait_ge(scaled, c + 1)
                dve.wait_ge(x1_stored[s], 16 * times)
                dve.wait_ge(t_done, c + 1)
                for j in range(CH):
                    last = nc.vector.tensor_scalar(x1_sb[s][:, j, :], x_sum[s][:, j, :], mv[s][:, j, 0:1], sd[s][:, j:j + 1],
                                                   ALU.subtract, ALU.mult)
                last.then_inc(x1_ready, 1)

            dve.sem_inc(hd_done, 1)
            dve.sem_inc(summed, 4)
            dve.sem_inc(x1_ready, 2)
            dve.wait_ge(w_loaded, 32)
            with dve.Fori(0, CHUNKS // 2) as i:
                for s in range(2):
                    c = 2 * i + s
                    dve.wait_ge(x_loaded[s], 16 * (i + 1))
                    dve.wait_ge(x1_ready, c + 1)
                    hu = HU[:, ds(c * CH * UW, CH * UW)].rearrange("p (j n) -> p j n", j=CH)[:, :, 0:D]
                    nc.vector.scalar_tensor_tensor(out=x_sum[s][:, :, :], in0=hu, scalar=0.0, in1=x_in[s][:, :, :],
                                                   op0=ALU.max, op1=ALU.add).then_inc(summed, 1)
                    dve.wait_ge(summed, 4 + 2 * c + 1)
                    layer_norm_stats(nc, dve, x_sum[s], stats, mv[s], summed, 4 + 2 * c + 1, stats_ready, passed)
                    if s == 0:
                        with dve.If(i > 0):
                            normalise(chunk(nc, dve, c - 1), 1, i)
                            project(chunk(nc, dve, c - 2))
                    else:
                        normalise(c - 1, 0, i + 1)
                        with dve.If(i > 0):
                            project(chunk(nc, dve, c - 2))
            normalise(CHUNKS - 1, 1, CHUNKS // 2)
            project(CHUNKS - 2)
            project(CHUNKS - 1)

        @block.scalar
        def _(act):
            def finish(c, s, times):
                act.wait_ge(x1_ready, 2 + c + 1)
                act.dma_start(x1[ds(c * P, P), :], x1_sb[s][:, :, :].rearrange("p j f -> p (j f)")).then_inc(x1_stored[s], 16)
                act.wait_ge(t_done, 2 + c + 1)
                act.wait_ge(x1T_stored[s], 16 * times)
                nc.scalar.activation(x1T_sb[s][:, :], tps, ACT.Copy).then_inc(xT_ready, 1)
                act.wait_ge(xT_ready, c + 1)
                act.dma_start(x1T[:, ds(c * CH * P, CH * P)], x1T_sb[s][:, :]).then_inc(x1T_stored[s], 16)
                act.wait_ge(h_done, c + 1)
                act.wait_ge(hs_stored[s], 16 * times)
                nc.scalar.activation(hs_sb[s][:, :, :], hs_ps, ACT.Copy).then_inc(hs_ready, 1)
                act.wait_ge(hs_ready, 1 + c + 1)
                act.dma_start(rows(hs, c), hs_sb[s][:, :, :]).then_inc(hs_stored[s], 16)

            with act.Fori(0, CHUNKS // 2) as i:
                for s in range(2):
                    c = 2 * i + s
                    act.wait_ge(stats_ready, c + 1)
                    nc.scalar.activation(sd[s][:, :], mv[s][:, :, 1], ACT.Sqrt, bias=eps[:, :]).then_inc(sd_ready, 1)
                    if s == 0:
                        with act.If(i > 0):
                            finish(chunk(nc, act, c - 1), 1, i)
                    else:
                        finish(c - 1, 0, i + 1)
            finish(CHUNKS - 1, 1, CHUNKS // 2)
            for s in range(2):
                act.wait_ge(x1_stored[s], 16 * (CHUNKS // 2 + 1))
                act.wait_ge(x1T_stored[s], 16 * (CHUNKS // 2 + 1))
                act.wait_ge(hs_stored[s], 16 * (CHUNKS // 2 + 1))

        @block.tensor
        def _(pe):
            pe.sem_inc(t_done, 2)
            pe.sem_inc(hs_ready, 1)
            pe.wait_ge(w_loaded, 32)
            with pe.Fori(0, CHUNKS // 2) as i:
                for s in range(2):
                    c = 2 * i + s
                    pe.wait_ge(x1_ready, 2 + c + 1)
                    for j in range(CH):
                        last = nc.tensor.transpose(tps[:, j * P:(j + 1) * P], x1_sb[s][:, j, :], ident[:, :])
                    last.then_inc(t_done, 1)
                    pe.wait_ge(xT_ready, c + 1)
                    pe.wait_ge(hs_ready, c + 1)
                    pe.wait_ge(hd_done, c + 1)
                    for j in range(CH):
                        xT = x1T_sb[s][:, j * P:(j + 1) * P]
                        nc.tensor.matmul(hs_ps[:, j, :], xT, w_sb[:, 0:D], start=True, stop=True)
                        last = nc.tensor.matmul(hd_ps[:, j, :], xT, w_sb[:, D:2 * D], start=True, stop=True)
                    last.then_inc(h_done, 1)


def phase_messages(nc, keep, meta, edges, ab, w1e, hs):
    rng, HU, Hd, iota_row = keep["rng"], keep["HU"], keep["Hd"], keep["iota_row"]
    neg_kb, node_id, ones2, ps = keep["neg_kb"], keep["node_id"], keep["ones2"], keep["ps"]
    with ExitStack() as stack:
        b = Build(nc, stack)
        w1e_sb = b.sb("w1e_sb", [P, 2 * D])
        meta_sb = [b.sb(f"mmeta_sb{i}", [P, 3, HC], I32) for i in range(2)]
        dstf = [b.sb(f"mdstf{i}", [P, HC]) for i in range(2)]
        ea = [b.sb(f"ea{i}", [P, GE // 2]) for i in range(RING)]
        ab_sb = [b.sb(f"mab{i}", [P, GE], BF16) for i in range(RING)]
        S = [b.sb(f"mS{i}", [P, GE]) for i in range(2)]
        S_x = b.sb("mS_x", [P, GE])
        rel = [b.sb(f"mrel{i}", [P, GROUP]) for i in range(2)]
        rel_x = b.sb("mrel_x", [P, GROUP])
        ST = b.sb("ST", [P, GE])
        ST_x = b.sb("ST_x", [P, GE])
        G = [b.sb(f"mG{i}", [P, GE]) for i in range(RING)]
        pre = [b.sb(f"pre{i}", [P, GE]) for i in range(2)]
        A = [b.sb(f"A{i}", [P, GROUP, UW]) for i in range(2)]
        h_ps = [ps[:, 0:GE], ps[:, GE:2 * GE]]
        bc = ps[:, 2 * GE:3 * GE]
        acc, acc_x = ps[:, 3 * GE:3 * GE + UW], ps[:, 3 * GE + 512:3 * GE + 512 + UW]

        w_loaded = b.sem("w1e_loaded")
        meta_loaded = [b.sem(f"mmeta_loaded{i}") for i in range(2)]
        dst_ready = b.sem("mdst_ready")
        ea_loaded = [b.sem(f"ea_loaded{i}") for i in range(RING)]
        ab_loaded = [b.sem(f"ab_loaded{i}") for i in range(RING)]
        ea_used = b.sem("ea_used")
        gathered = [b.sem(f"mgathered{i}") for i in range(RING)]
        bc_ready = b.sem("bc_ready")
        st_ready, h_ready = b.sem("st_ready"), b.sem("h_ready")
        s_ready = b.sem("ms_ready")
        h_added = b.sem("h_added")
        silu_done = b.sem("silu_done")
        agg_done = b.sem("magg_done")
        acc_free = b.sem("macc_free")
        stx_ready, hx_done = b.sem("stx_ready"), b.sem("hx_done")
        sx_ready, aggx_done = b.sem("msx_ready"), b.sem("maggx_done")
        rel_ready, relx_ready = b.sem("mrel_ready"), b.sem("mrelx_ready")
        addx_done = b.sem("maddx_done")
        a_ones, ab_zeroed, w_zeroed = b.sem("a_ones"), b.sem("ab_zeroed"), b.sem("w_zeroed")
        passed = keep["passed"]
        block = stack.enter_context(nc.Block())

        @block.gpsimd
        def _(pool):
            def gather(s):
                for u in range(GROUP):
                    col = (s % HALF) * GROUP + u
                    nc.gpsimd.indirect_dma_start(
                        out=G[s % RING][:, u * P:(u + 1) * P], out_offset=None, in_=hs,
                        in_offset=bass.IndirectOffsetOnAxis(ap=meta_sb[s // HALF][:, 0, col:col + 1], axis=0),
                    ).then_inc(gathered[s % RING], 16)

            with pool.Fori(0, BODIES) as i:
                for s in range(STEPS):
                    g = STEPS * i + s
                    if s % HALF == 0:
                        m = s // HALF
                        pool.wait_ge(meta_loaded[m], 16 * (i + 1))
                    wait_apart(pool, h_added, g + 1, passed)
                    gather(s)

        @block.sync
        def _(sp):
            sp.wait_ge(w_zeroed, 1)
            for half in range(2):
                sp.dma_start(w1e_sb[half * DE:(half + 1) * DE, half * D:(half + 1) * D], w1e).then_inc(w_loaded, 16)
            sp.wait_ge(ab_zeroed, RING)
            with sp.Fori(0, BODIES) as i:
                for s in range(STEPS):
                    g = STEPS * i + s
                    sp.wait_ge(ea_used, g + 1)
                    sp.dma_start(ea[s % RING][:, :], edges[ds(g), :, :].rearrange("o p e -> (o p) e")).then_inc(ea_loaded[s % RING], 16)
                    sp.dma_start(ab_sb[s % RING][0:2, :], ab[:, ds(g * GE, GE)]).then_inc(ab_loaded[s % RING], 16)

        @block.scalar
        def _(act):
            def load(h, m):
                act.dma_start(meta_sb[m][:, :, :], meta[ds(h), :, :, :].rearrange("o p a c -> (o p) a c")).then_inc(meta_loaded[m], 16)

            load(0, 0)
            act.sem_inc(silu_done, 2)
            act.wait_ge(a_ones, 2)
            with act.Fori(0, BODIES) as i:
                for s in range(STEPS):
                    g = STEPS * i + s
                    act.wait_ge(h_added, RING + g + 1)
                    nc.scalar.activation(A[s % 2][:, :, 0:D], pre[s % 2][:, :].rearrange("p (u f) -> p u f", u=GROUP),
                                         ACT.Silu).then_inc(silu_done, 1)
                    if s % HALF == 1:
                        m = s // HALF
                        load(2 * i + m + 1, 1 - m)

        @block.vector
        def _(dve):
            def prepare(m, times):
                dve.wait_ge(meta_loaded[m], 16 * times)
                nc.vector.tensor_copy(dstf[m][:, :], meta_sb[m][:, 2, :]).then_inc(dst_ready, 1)

            def one_hot(out, rel_t, ready, count, k, s):
                m, c0 = s // HALF, (s % HALF) * GROUP
                nc.vector.tensor_scalar(rel_t[:, :], dstf[m][:, c0:c0 + GROUP], neg_kb[:, ds(k)], None,
                                        ALU.add).then_inc(ready, 1)
                dve.wait_ge(ready, count)
                nodes = iota_row[:, :].rearrange("p (o n) -> p o n", o=1).to_broadcast([P, GROUP, P])
                dsts = rel_t[:, :].rearrange("p (u o) -> p u o", o=1).to_broadcast([P, GROUP, P])
                return nc.vector.tensor_tensor(out[:, :].rearrange("p (u n) -> p u n", u=GROUP), nodes, dsts, ALU.is_equal)

            def one_hot_T(out, k):
                return nc.vector.tensor_scalar(out[:, :], bc, node_id[:, ds(k)], None, ALU.is_equal)

            def extra_one_hot(base, k, s):
                one_hot(S_x, rel_x, relx_ready, base + k, k, s).then_inc(sx_ready, 1)

            def back_prepare(blocks, s):
                lo, hi, base = blocks
                with dve.If(lo < hi):
                    extra_one_hot(base, lo + 1, s)

            def back(g, blocks, s):
                lo, hi, base = blocks
                dve.wait_ge(agg_done, g + 1)
                nc.vector.tensor_tensor(HU[:, ds(lo * UW, UW)], HU[:, ds(lo * UW, UW)], acc, ALU.add).then_inc(acc_free, 1)
                with dve.If(lo < hi):
                    with dve.Fori(lo + 1, hi + 1) as k:
                        dve.wait_ge(aggx_done, base + k)
                        nc.vector.tensor_tensor(HU[:, ds(k * UW, UW)], HU[:, ds(k * UW, UW)], acc_x, ALU.add).then_inc(addx_done, 1)
                        wait_apart(dve, addx_done, base + k, passed)
                        with dve.If(k < hi):
                            extra_one_hot(base, k + 1, s)

            nc.vector.memset(w1e_sb[:, :], 0.0).then_inc(w_zeroed, 1)
            for t in A:
                nc.vector.memset(t[:, :, D:UW], 1.0).then_inc(a_ones, 1)
            for t in ab_sb:
                nc.vector.memset(t[:, :], 0.0).then_inc(ab_zeroed, 1)
            dve.sem_inc(s_ready, 1)
            dve.sem_inc(h_added, RING)
            dve.sem_inc(acc_free, 1)
            dve.sem_inc(stx_ready, CREDIT)
            dve.sem_inc(relx_ready, CREDIT)
            dve.sem_inc(sx_ready, CREDIT)
            dve.sem_inc(addx_done, CREDIT)
            prepare(0, 1)
            with dve.Fori(0, BODIES) as i:
                blocks = block_range(nc, dve, rng, STEPS * i)
                for s in range(STEPS):
                    g = STEPS * i + s
                    lo, hi, base = blocks
                    dve.wait_ge(bc_ready, g + 1)
                    one_hot_T(ST, lo).then_inc(st_ready, 1)
                    with dve.If(lo < hi):
                        with dve.Fori(lo + 1, hi + 1) as k:
                            dve.wait_ge(hx_done, base + k - 1)
                            one_hot_T(ST_x, k).then_inc(stx_ready, 1)
                    if s % HALF == 0:
                        dve.wait_ge(dst_ready, 2 * i + s // HALF + 1)
                    one_hot(S[s % 2], rel[s % 2], rel_ready, g + 1, lo, s).then_inc(s_ready, 1)
                    if s == 0:
                        with dve.If(i > 0):
                            back_prepare(block_range(nc, dve, rng, g - 1), STEPS - 1)
                    else:
                        back_prepare(before, s - 1)
                    if s < STEPS - 1:
                        following = block_range(nc, dve, rng, g + 1)
                    wait_apart(dve, h_ready, g + 1, passed)
                    with dve.If(lo < hi):
                        wait_apart(dve, hx_done, base + hi, passed)
                    dve.wait_ge(gathered[s % RING], 16 * GROUP * (STEPS // RING * i + s // RING + 1))
                    dve.wait_ge(silu_done, g + 1)
                    nc.vector.tensor_tensor(pre[s % 2][:, :], h_ps[s % 2], G[s % RING][:, :], ALU.add).then_inc(h_added, 1)
                    if s == 0:
                        with dve.If(i > 0):
                            back(g - 1, block_range(nc, dve, rng, g - 1), STEPS - 1)
                    else:
                        back(g - 1, before, s - 1)
                    if s % HALF == 3:
                        m = s // HALF
                        prepare(1 - m, i + 1 + m)
                    before, blocks = blocks, following
            last_blocks = block_range(nc, dve, rng, GROUPS - 1)
            back_prepare(last_blocks, STEPS - 1)
            back(GROUPS - 1, last_blocks, STEPS - 1)

        @block.tensor
        def _(pe):
            pe.sem_inc(ea_used, RING)
            pe.sem_inc(hx_done, CREDIT)
            pe.sem_inc(aggx_done, CREDIT)
            pe.wait_ge(w_loaded, 32)

            def edge_part(s):
                for v in range(GROUP // 2):
                    last = nc.tensor.matmul(h_ps[s % 2][:, 2 * v * P:2 * (v + 1) * P], ea[s % RING][:, v * P:(v + 1) * P],
                                            w1e_sb[:, :], start=(2 * v * P % BANK == 0), stop=False, skip_group_check=True)
                return last

            def dst_part(onehot_T, k, s):
                for u in range(GROUP):
                    last = nc.tensor.matmul(h_ps[s % 2][:, u * P:(u + 1) * P], onehot_T[:, u * P:(u + 1) * P],
                                            Hd[:, ds(k * D, D)], start=False, stop=True, skip_group_check=True)
                return last

            def aggregate(out, onehot, s):
                for u in range(GROUP):
                    last = nc.tensor.matmul(out, onehot[:, u * P:(u + 1) * P], A[s % 2][:, u, :],
                                            start=(u == 0), stop=(u == GROUP - 1))
                return last

            def back(g, blocks, s):
                lo, hi, base = blocks
                pe.wait_ge(silu_done, 2 + g + 1)
                pe.wait_ge(s_ready, 1 + g + 1)
                pe.wait_ge(acc_free, g + 1)
                aggregate(acc, S[s % 2], s).then_inc(agg_done, 1)
                with pe.If(lo < hi):
                    with pe.Fori(lo + 1, hi + 1) as k:
                        pe.wait_ge(sx_ready, base + k)
                        aggregate(acc_x, S_x, s).then_inc(aggx_done, 1)

            with pe.Fori(0, BODIES) as i:
                for s in range(STEPS):
                    g = STEPS * i + s
                    times = STEPS // RING * i + s // RING + 1
                    pe.wait_ge(ab_loaded[s % RING], 16 * times)
                    pe.wait_ge(s_ready, g + 1)
                    for half in range(2):
                        cols = slice(half * GE // 2, (half + 1) * GE // 2)
                        last = nc.tensor.matmul(bc[:, cols], ones2[:, :], ab_sb[s % RING][:, cols], start=True, stop=True)
                    last.then_inc(bc_ready, 1)
                    pe.wait_ge(ea_loaded[s % RING], 16 * times)
                    pe.wait_ge(h_added, g + RING - 1)
                    edge_part(s).then_inc(ea_used, 1)
                    blocks = block_range(nc, pe, rng, g)
                    lo, hi, base = blocks
                    pe.wait_ge(st_ready, g + 1)
                    dst_part(ST, lo, s).then_inc(h_ready, 1)
                    with pe.If(lo < hi):
                        with pe.Fori(lo + 1, hi + 1) as k:
                            pe.wait_ge(stx_ready, base + k)
                            dst_part(ST_x, k, s).then_inc(hx_done, 1)
                    if s == 0:
                        with pe.If(i > 0):
                            back(g - 1, block_range(nc, pe, rng, g - 1), STEPS - 1)
                    else:
                        back(g - 1, before, s - 1)
                    before = blocks
            back(GROUPS - 1, block_range(nc, pe, rng, GROUPS - 1), STEPS - 1)


def phase_update(nc, keep, x1, x1T, out):
    HU, ps, ident, eps = keep["HU"], keep["ps"], keep["ident"], keep["eps"]
    top, w2b, b2b = keep["top"], keep["w2b"], keep["b2b"]
    bgt_sb, gamma_sb, beta_sb = keep["bgt"], keep["gamma"], keep["beta"]
    with ExitStack() as stack:
        b = Build(nc, stack)
        per_edge = b.sb("per_edge", [P, BLOCKS])
        has = b.sb("has", [P, BLOCKS])

        def pair(name, shape):
            return [b.sb(f"{name}{s}", shape) for s in range(2)]

        x1_sb, x1b = pair("x1_sb", [P, CH, D]), pair("x1b", [P, CH, D])
        x1T_sb, VT = pair("ux1T_sb", [P, CH * P]), pair("VT", [P, CH * P])
        V = pair("V", [P, CH, D])
        zb, z = pair("zb", [P, CH, 2 * D]), pair("z", [P, CH, 2 * D])
        u = pair("u", [P, CH, D])
        y, result = pair("y", [P, CH, D]), pair("result", [P, CH, D])
        mv1, sd1, shift1 = pair("mv1_", [P, CH, 2]), pair("sd1_", [P, CH]), pair("shift1_", [P, CH])
        mv2, sd2, shift2 = pair("mv2_", [P, CH, 2]), pair("sd2_", [P, CH]), pair("shift2_", [P, CH])
        stats = pair("ustats", [P, CH, 6])
        tps = ps[:, 0:CH * P]
        zps = ps[:, 1024:1024 + CH * 2 * D].rearrange("p (j n) -> p j n", j=CH)

        x1_loaded = [b.sem(f"ux1_loaded{i}") for i in range(2)]
        x1T_loaded = [b.sem(f"ux1T_loaded{i}") for i in range(2)]
        out_stored = [b.sem(f"out_stored{i}") for i in range(2)]
        counts_ready = b.sem("counts_ready")
        v_ready, zb_ready, x1b_ready = b.sem("v_ready"), b.sem("zb_ready"), b.sem("x1b_ready")
        t_done = b.sem("ut_done")
        vT_ready = b.sem("vT_ready")
        z_done = b.sem("z_done")
        z_ready = b.sem("z_ready")
        gates = b.sem("gates")
        maxed = b.sem("maxed")
        zb_part = b.sem("zb_part")
        gated, normed = b.sem("gated"), b.sem("normed")
        stats1_ready, stats2_ready = b.sem("stats1_ready"), b.sem("stats2_ready")
        sd1_ready, sd2_ready = b.sem("sd1_ready"), b.sem("sd2_ready")
        scale1_ready, scale2_ready = b.sem("scale1_ready"), b.sem("scale2_ready")
        y_ready = b.sem("y_ready")
        out_ready = b.sem("out_ready")
        GATED, NORMED = 4, 3
        passed = keep["passed"]
        block = stack.enter_context(nc.Block())

        def rows(dram, c):
            return dram[ds(c * CH * P, CH * P), :].rearrange("(j p) f -> p j f", p=P)

        def over_blocks(row):
            return row[:, :].rearrange("p (o f) -> p o f", o=1).to_broadcast([P, CH, row.shape[-1]])

        @block.sync
        def _(sp):
            for s in range(2):
                sp.sem_inc(out_stored[s], 16)

            def load_x1(c, s):
                sp.wait_ge(stats1_ready, c + 1)
                sp.wait_ge(x1b_ready, c + 1)
                sp.dma_start(x1_sb[s][:, :, :].rearrange("p j f -> p (j f)"), x1[ds(c * P, P), :]).then_inc(x1_loaded[s], 16)

            with sp.Fori(0, CHUNKS // 2) as i:
                for s in range(2):
                    c = 2 * i + s
                    sp.wait_ge(z_done, c + 1)
                    sp.dma_start(x1T_sb[s][:, :], x1T[:, ds(c * CH * P, CH * P)]).then_inc(x1T_loaded[s], 16)
                    if s == 0:
                        with sp.If(i > 0):
                            load_x1(chunk(nc, sp, c - 1), 1)
                    else:
                        load_x1(c - 1, 0)
            load_x1(CHUNKS - 1, 1)

        @block.gpsimd
        def _(pool):
            def messages(c, s):
                hu = HU[:, ds(c * CH * UW, CH * UW)].rearrange("p (j n) -> p j n", j=CH)
                scale = per_edge[:, ds(c * CH, CH)].rearrange("p (j o) -> p j o", o=1).to_broadcast([P, CH, D])
                pool.wait_ge(t_done, c + 1)
                nc.gpsimd.tensor_tensor(V[s][:, :, :], hu[:, :, 0:D], scale, ALU.mult).then_inc(v_ready, 1)
                pool.wait_ge(z_ready, c + 1)
                own = has[:, ds(c * CH, CH)].rearrange("p (j o) -> p j o", o=1).to_broadcast([P, CH, 2 * D])
                nc.gpsimd.tensor_tensor(zb[s][:, :, :], over_blocks(b2b), own, ALU.mult).then_inc(zb_part, 1)
                pool.wait_ge(zb_part, c + 1)
                nc.gpsimd.tensor_tensor(zb[s][:, :, :], zb[s][:, :, :], over_blocks(bgt_sb), ALU.add).then_inc(zb_ready, 1)

            def add_beta(c, s, times):
                pool.wait_ge(x1_loaded[s], 16 * times)
                pool.wait_ge(stats2_ready, c + 1)
                nc.gpsimd.tensor_tensor(x1b[s][:, :, :], x1_sb[s][:, :, :], over_blocks(beta_sb), ALU.add).then_inc(x1b_ready, 1)

            pool.sem_inc(x1b_ready, 2)
            pool.wait_ge(counts_ready, 2)
            messages(0, 0)
            with pool.Fori(0, CHUNKS // 2) as i:
                for s in range(2):
                    c = 2 * i + s
                    if s == 0:
                        messages(c + 1, 1)
                        with pool.If(i > 0):
                            add_beta(chunk(nc, pool, c - 1), 1, i)
                    else:
                        with pool.If(i < CHUNKS // 2 - 1):
                            messages(chunk(nc, pool, c + 1), 0)
                        add_beta(c - 1, 0, i + 1)
            add_beta(CHUNKS - 1, 1, CHUNKS // 2)

        @block.tensor
        def _(pe):
            pe.sem_inc(t_done, 2)
            pe.sem_inc(z_done, 2)
            with pe.Fori(0, CHUNKS // 2) as i:
                for s in range(2):
                    c = 2 * i + s
                    pe.wait_ge(v_ready, c + 1)
                    for j in range(CH):
                        last = nc.tensor.transpose(tps[:, j * P:(j + 1) * P], V[s][:, j, :], ident[:, :])
                    last.then_inc(t_done, 1)
                    pe.wait_ge(x1T_loaded[s], 16 * (i + 1))
                    pe.wait_ge(vT_ready, c + 1)
                    pe.wait_ge(z_ready, c + 2)
                    for j in range(CH):
                        nc.tensor.matmul(zps[:, j, :], x1T_sb[s][:, j * P:(j + 1) * P], top[:, :], start=True, stop=False)
                        last = nc.tensor.matmul(zps[:, j, :], VT[s][:, j * P:(j + 1) * P], w2b[:, :], start=False, stop=True)
                    last.then_inc(z_done, 1)

        @block.scalar
        def _(act):
            def copy_T(c, s):
                act.wait_ge(t_done, 2 + c + 1)
                nc.scalar.activation(VT[s][:, :], tps, ACT.Copy).then_inc(vT_ready, 1)

            def last_norm(c, s, times):
                act.wait_ge(scale2_ready, 2 * c + 2)
                act.wait_ge(out_stored[s], 16 * times)
                for j in range(CH):
                    last = nc.scalar.activation(result[s][:, j, :], y[s][:, j, :], ACT.Identity,
                                                scale=sd2[s][:, j:j + 1], bias=shift2[s][:, j:j + 1])
                last.then_inc(out_ready, 1)
                act.wait_ge(out_ready, 2 + c + 1)
                act.dma_start(rows(out, c), result[s][:, :, :]).then_inc(out_stored[s], 16)

            def first_norm(c, s):
                act.wait_ge(scale1_ready, 2 * c + 2)
                act.wait_ge(out_ready, c + 1)
                for j in range(CH):
                    last = nc.scalar.activation(y[s][:, j, :], u[s][:, j, :], ACT.Identity,
                                                scale=sd1[s][:, j:j + 1], bias=shift1[s][:, j:j + 1])
                last.then_inc(y_ready, 1)

            def deviation(stats_ready, sd, mv, ready, c):
                act.wait_ge(stats_ready, 2 + c + 1)
                nc.scalar.activation(sd[:, :], mv[:, :, 1], ACT.Sqrt, bias=eps[:, :]).then_inc(ready, 1)

            def deviation1(c, s):
                deviation(stats1_ready, sd1[s], mv1[s], sd1_ready, c)

            def deviation2(c, s):
                deviation(stats2_ready, sd2[s], mv2[s], sd2_ready, c)

            act.sem_inc(out_ready, 2)
            copy_T(0, 0)
            with act.Fori(0, CHUNKS // 2) as i:
                for s in range(2):
                    c = 2 * i + s
                    if s == 0:
                        copy_T(c + 1, 1)
                    else:
                        with act.If(i < CHUNKS // 2 - 1):
                            copy_T(c + 1, 0)
                    act.wait_ge(z_ready, 2 + c + 1)
                    nc.scalar.activation(z[s][:, :, 0:D], z[s][:, :, 0:D], ACT.Tanh, scale=0.5).then_inc(gates, 1)
                    nc.scalar.activation(z[s][:, :, D:2 * D], z[s][:, :, D:2 * D], ACT.Tanh).then_inc(gates, 1)
                    with act.If(i > 0):
                        first_norm(chunk(nc, act, c - 2), s)
                    with act.If(i > 1 - s):
                        last_norm(chunk(nc, act, c - 3), 1 - s, chunk(nc, act, i + s - 1))
                    if s == 0:
                        with act.If(i > 0):
                            deviation1(chunk(nc, act, c - 1), 1)
                            deviation2(chunk(nc, act, c - 2), 0)
                    else:
                        deviation1(c - 1, 0)
                        with act.If(i > 0):
                            deviation2(chunk(nc, act, c - 2), 1)
            first_norm(CHUNKS - 2, 0)
            last_norm(CHUNKS - 3, 1, CHUNKS // 2 - 1)
            deviation1(CHUNKS - 1, 1)
            deviation2(CHUNKS - 2, 0)
            first_norm(CHUNKS - 1, 1)
            last_norm(CHUNKS - 2, 0, CHUNKS // 2)
            deviation2(CHUNKS - 1, 1)
            last_norm(CHUNKS - 1, 1, CHUNKS // 2)
            for s in range(2):
                act.wait_ge(out_stored[s], 16 * (CHUNKS // 2 + 1))

        @block.vector
        def _(dve):
            def update(c, s, times):
                then = stepper(dve, gated, GATED * c)
                uc, gate, tr = u[s][:, :, :], z[s][:, :, 0:D], z[s][:, :, D:2 * D]
                dve.wait_ge(gates, 2 * c + 2)
                dve.wait_ge(x1_loaded[s], 16 * times)
                then(nc.vector.tensor_tensor(uc, x1_sb[s][:, :, :], tr, ALU.subtract))
                then(nc.vector.scalar_tensor_tensor(out=uc, in0=gate, scalar=1.0, in1=uc, op0=ALU.add, op1=ALU.mult))
                then(nc.vector.scalar_tensor_tensor(out=uc, in0=uc, scalar=0.5, in1=tr, op0=ALU.mult, op1=ALU.add))
                layer_norm_stats(nc, dve, u[s], stats[0], mv1[s], gated, GATED * c + 3, stats1_ready, passed)

            def residual(c, s):
                then = stepper(dve, normed, NORMED * c)
                dve.wait_ge(y_ready, c + 1)
                then(nc.vector.tensor_tensor(y[s][:, :, :], y[s][:, :, :], over_blocks(gamma_sb), ALU.mult))
                dve.wait_ge(x1b_ready, 2 + c + 1)
                then(nc.vector.tensor_tensor(y[s][:, :, :], y[s][:, :, :], x1b[s][:, :, :], ALU.add))
                layer_norm_stats(nc, dve, y[s], stats[1], mv2[s], normed, NORMED * c + 2, stats2_ready, passed)

            def scale(sd_ready, sd, mv, shift, ready, c):
                dve.wait_ge(sd_ready, c + 1)
                nc.vector.reciprocal(sd[:, :], sd[:, :]).then_inc(ready, 1)
                dve.wait_ge(ready, 2 * c + 1)
                nc.vector.scalar_tensor_tensor(out=shift[:, :], in0=mv[:, :, 0], scalar=-1.0, in1=sd[:, :],
                                               op0=ALU.mult, op1=ALU.mult).then_inc(ready, 1)

            def scale1(c, s):
                scale(sd1_ready, sd1[s], mv1[s], shift1[s], scale1_ready, c)

            def scale2(c, s):
                scale(sd2_ready, sd2[s], mv2[s], shift2[s], scale2_ready, c)

            dve.sem_inc(z_ready, 2)
            dve.sem_inc(stats1_ready, 2)
            dve.sem_inc(stats2_ready, 2)
            counts = HU[:, :].rearrange("p (k n) -> p k n", k=BLOCKS)[:, :, D]
            nc.vector.tensor_scalar(has[:, :], counts, 1.0, None, ALU.min).then_inc(counts_ready, 1)
            nc.vector.tensor_scalar(per_edge[:, :], counts, 1.0, None, ALU.max).then_inc(maxed, 1)
            dve.wait_ge(maxed, 1)
            nc.vector.reciprocal(per_edge[:, :], per_edge[:, :]).then_inc(counts_ready, 1)
            with dve.Fori(0, CHUNKS // 2) as i:
                for s in range(2):
                    c = 2 * i + s
                    dve.wait_ge(zb_ready, c + 1)
                    dve.wait_ge(z_done, 2 + c + 1)
                    nc.vector.tensor_tensor(z[s][:, :, :], zps, zb[s][:, :, :], ALU.add).then_inc(z_ready, 1)
                    with dve.If(i > 0):
                        scale1(chunk(nc, dve, c - 2), s)
                    with dve.If(i > 1 - s):
                        scale2(chunk(nc, dve, c - 3), 1 - s)
                    if s == 0:
                        with dve.If(i > 0):
                            update(chunk(nc, dve, c - 1), 1, i)
                            residual(chunk(nc, dve, c - 2), 0)
                    else:
                        update(c - 1, 0, i + 1)
                        with dve.If(i > 0):
                            residual(chunk(nc, dve, c - 2), 1)
            scale1(CHUNKS - 2, 0)
            scale2(CHUNKS - 3, 1)
            update(CHUNKS - 1, 1, CHUNKS // 2)
            residual(CHUNKS - 2, 0)
            scale1(CHUNKS - 1, 1)
            scale2(CHUNKS - 2, 0)
            residual(CHUNKS - 1, 1)
            scale2(CHUNKS - 1, 1)


def build_program(nc, x, xT, meta, wts, dst_tiles, dst_rows, edges, w0, w1sd, w1e, b1, w2T, b2, wgt_top, wgt_bot,
                  bgt, gamma, beta, out):
    hr = nc.dram_tensor("hr", (NPAD * NREL, D), F32).ap()
    hs = nc.dram_tensor("hs", (NPAD, D), F32).ap()
    x1 = nc.dram_tensor("x1", (CHUNKS * P, CH * D), F32).ap()
    x1T = nc.dram_tensor("x1T", (D, NPAD), F32).ap()
    ab = nc.dram_tensor("ab", (2, EPAD), BF16).ap()
    with ExitStack() as stack:
        b = Build(nc, stack)
        keep = {
            "rng": b.sb("rng", [1, GROUPS + 1], I32),
            "HU": b.sb("HU", [P, BLOCKS * UW]),
            "iota_row": b.sb("iota_row", [P, P]),
            "neg_kb": b.sb("neg_kb", [P, BLOCKS + 1]),
            "node_id": b.sb("node_id", [P, BLOCKS]),
            "pid_i": b.sb("pid_i", [P, BLOCKS], I32),
            "ones2": b.sb("ones2", [P, P], BF16),
            "ident": b.sb("ident", [P, P]),
            "w2b": b.sb("w2b", [P, 2 * D]),
            "b2b": b.sb("b2b", [P, 2 * D]),
            "top": b.sb("top", [P, 2 * D]),
            "bgt": b.sb("bgt_sb", [P, 2 * D]),
            "gamma": b.sb("gamma_sb", [P, D]),
            "beta": b.sb("beta_sb", [P, D]),
            "eps": b.sb("eps", [P, 1]),
            "passed": b.sem("passed"),
            "ps": stack.enter_context(nc.psum_tensor("ps", [P, 4096], F32)),
        }
        phase_tables(nc, keep, xT, w0, dst_tiles, hr)
        phase_relational(nc, keep, meta, wts, hr, dst_rows, ab, (w2T, wgt_top, wgt_bot, b2, bgt, gamma, beta))
        keep["Hd"] = b.sb("Hd", [P, BLOCKS * D])
        phase_nodes(nc, keep, x, w1sd, b1, x1, x1T, hs)
        phase_messages(nc, keep, meta, edges, ab, w1e, hs)
        phase_update(nc, keep, x1, x1T, out)


def kernel(x, src, dst, edge_attr_64, edge_type_3, edge_weight, L0_gnn_weight, L1_gnn_W1, L1_gnn_b1, L1_gnn_W2,
           L1_gnn_b2, L1_gnn_Wg, L1_gnn_bg, L1_gnn_Wt, L1_gnn_bt, L1_gnn_gamma, L1_gnn_beta):
    import numpy as np
    from concourse import bacc
    from concourse.bass_utils import run_bass_kernel_spmd

    def padded(a, n, value=0):
        a = np.asarray(a)
        return np.concatenate([a, np.full((n - a.shape[0], *a.shape[1:]), value, a.dtype)])

    def by_half(a):
        return a.reshape(-1, HC, P).transpose(0, 2, 1)

    more = EPAD + HC * P
    src_p, typ_p = padded(src, more), padded(edge_type_3, more)
    dst_p = padded(dst, more, NPAD - 1)
    x_p = padded(x, NPAD)
    arrays = {
        "x": x_p,
        "xT": x_p.reshape(CHUNKS, P, CH, D).transpose(3, 0, 2, 1).reshape(D, NPAD),
        "meta": np.stack([by_half(src_p), by_half(typ_p), by_half(dst_p)], axis=2),
        "wts": by_half(padded(edge_weight, more)),
        "dst_tiles": dst_p[:EPAD].reshape(TILES, P).T,
        "dst_rows": dst_p[:EPAD].reshape(P, TILES),
        "edges": padded(edge_attr_64, EPAD).reshape(GROUPS, GROUP // 2, 2, P, DE).transpose(0, 2, 4, 1, 3).reshape(GROUPS, P, GE // 2),
        "w0": np.asarray(L0_gnn_weight).transpose(1, 0, 2).reshape(D, NREL * D),
        "w1sd": np.concatenate([np.asarray(L1_gnn_W1)[0:D], np.asarray(L1_gnn_W1)[D:2 * D]], axis=1),
        "w1e": np.asarray(L1_gnn_W1)[2 * D:],
        "b1": np.asarray(L1_gnn_b1).reshape(1, D),
        "w2T": np.asarray(L1_gnn_W2).T,
        "b2": np.asarray(L1_gnn_b2).reshape(D, 1),
        "wgt_top": np.concatenate([np.asarray(L1_gnn_Wg)[0:D], np.asarray(L1_gnn_Wt)[0:D]], axis=1),
        "wgt_bot": np.concatenate([np.asarray(L1_gnn_Wg)[D:], np.asarray(L1_gnn_Wt)[D:]], axis=1),
        "bgt": np.concatenate([np.asarray(L1_gnn_bg), np.asarray(L1_gnn_bt)]).reshape(1, 2 * D),
        "gamma": np.asarray(L1_gnn_gamma).reshape(1, D),
        "beta": np.asarray(L1_gnn_beta).reshape(1, D),
    }
    arrays = {name: np.ascontiguousarray(a) for name, a in arrays.items()}
    nc = bacc.Bacc("TRN2", target_bir_lowering=False, num_devices=1)
    args = [nc.dram_tensor(f"in_{n}", a.shape, mybir.dt.from_np(a.dtype), kind="ExternalInput").ap() for n, a in arrays.items()]
    out = nc.dram_tensor("out_0", (NPAD, D), F32, kind="ExternalOutput").ap()
    build_program(nc, *args, out)
    r = run_bass_kernel_spmd(nc, [{f"in_{n}": a for n, a in arrays.items()}], core_ids=[0])
    return r.results[0]["out_0"][:NODES]
```
